# Optimizing a Trainium2 kernel written in Bass

```python
import numpy as np
import jax
import jax.numpy as jnp

def _softmax(x, axis=-1):
    return jax.nn.softmax(x, axis=axis)

def _gelu(x):
    return jax.nn.gelu(x, approximate=True)

def _silu(x):
    return jax.nn.silu(x)

def _sigmoid(x):
    return jax.nn.sigmoid(x)

def _layernorm(x, axis=-1, eps=1e-05):
    m = jnp.mean(x, axis=axis, keepdims=True)
    v = jnp.var(x, axis=axis, keepdims=True)
    return (x - m) / jnp.sqrt(v + eps)

def _scatter_add(tgt, idx, src, axis=0):
    return tgt.at[idx].add(src)

def _segment_sum(src, seg, n):
    return jax.ops.segment_sum(src, seg, n)
kernel_name = 'mk_early_fusion_d1_tok_img512_r4_4e34ba'

def setup_inputs(seed: int=0):
    np.random.seed(seed)
    _w = jnp.asarray

    def _rec_inputs():
        import jax
        import jax.numpy as jnp
        _rk = jax.random.key(seed)
        x = 7.57192e-06 + 1.00007 * jax.random.normal(jax.random.fold_in(_rk, 1), (8, 518, 518, 3), jnp.float32)
        txt = -0.000319884 + 0.450765 * jax.random.normal(jax.random.fold_in(_rk, 2), (8, 77, 128), jnp.float32)
        return (x, txt)
    x, txt = _rec_inputs()

    def _L0_tok_setup():
        import jax, jax.numpy as jnp
        import numpy as np
        B, H, W, C = (64, 224, 224, 3)
        P, D = (16, 128)
        LN_EPS = 0.001

        def _shift4(x):
            pad = lambda a, spec: jnp.pad(a, spec)
            right = pad(x[:, :, :-1, :], ((0, 0), (0, 0), (1, 0), (0, 0)))
            left = pad(x[:, :, 1:, :], ((0, 0), (0, 0), (0, 1), (0, 0)))
            down = pad(x[:, :-1, :, :], ((0, 0), (1, 0), (0, 0), (0, 0)))
            up = pad(x[:, 1:, :, :], ((0, 0), (0, 1), (0, 0), (0, 0)))
            return [right, left, down, up]
        key = jax.random.key(seed)
        k0, k1, k2 = jax.random.split(key, 3)
        x = jax.random.normal(k0, (B, H, W, C), jnp.float32)
        conv_w = jax.random.normal(k1, (P, P, 5 * C, D), jnp.float32) * 0.02
        conv_b = jnp.zeros((D,), jnp.float32)
        gamma = jnp.ones((D,), jnp.float32)
        beta = jnp.zeros((D,), jnp.float32)
        dense_w = jax.random.normal(k2, (D, D), jnp.float32) * 0.02
        dense_b = jnp.zeros((D,), jnp.float32)
        return {'x': x, 'conv_w': conv_w, 'conv_b': conv_b, 'gamma': gamma, 'beta': beta, 'dense_w': dense_w, 'dense_b': dense_b}
    _L0_tok_all = _L0_tok_setup()
    _L0_tok_in = {k: v for k, v in _L0_tok_all.items() if k in ('conv_w', 'conv_b', 'gamma', 'beta', 'dense_w', 'dense_b')}
    del _L0_tok_all

    def _L0_attn_setup():
        import jax, jax.numpy as jnp
        import numpy as np
        N_HEADS = 8
        D_K = 64
        NEG = 1000000000.0
        key = jax.random.key(seed)
        k1, k2, k3 = jax.random.split(key, 3)
        B, L, C = (4, 512, 128)
        x = jax.random.normal(k1, (B, L, C), dtype=jnp.float32)
        W_in = jax.random.normal(k2, (C, N_HEADS * D_K * 3), dtype=jnp.float32) * C ** (-0.5)
        b_in = jnp.zeros((N_HEADS * D_K * 3,), dtype=jnp.float32)
        W_out = jax.random.normal(k3, (N_HEADS * D_K, C), dtype=jnp.float32) * (N_HEADS * D_K) ** (-0.5)
        b_out = jnp.zeros((C,), dtype=jnp.float32)
        return {'x': x, 'W_in': W_in, 'b_in': b_in, 'W_out': W_out, 'b_out': b_out}
    _L0_attn_all = _L0_attn_setup()
    _L0_attn_in = {k: v for k, v in _L0_attn_all.items() if k in ('W_in', 'b_in', 'W_out', 'b_out')}
    del _L0_attn_all

    def _L0_ffn_setup():
        import jax, jax.numpy as jnp
        import numpy as np
        from jax import lax
        N, M, DIM, HEADS, TOPK = (4, 512, 128, 8, 16)

        def _split_heads(t, h):
            n, m, c = t.shape
            return t.reshape(n, m, h, c // h).transpose(0, 2, 1, 3).reshape(n * h, m, c // h)
        key = jax.random.key(seed)
        ks = jax.random.split(key, 7)
        f = lambda k, s, sc=1.0: jax.random.normal(k, s, dtype=jnp.float32) * sc
        return {'x': f(ks[0], (N, M, DIM)), 'pos_w': f(ks[1], (DIM, 1, 3), 0.1), 'pos_b': f(ks[2], (DIM,), 0.02), 'qkv_w': f(ks[3], (3 * DIM, DIM), 0.02), 'qkv_b': f(ks[4], (3 * DIM,), 0.02), 'wo_w': f(ks[5], (DIM, DIM), 0.02), 'wo_b': f(ks[6], (DIM,), 0.02)}
    _L0_ffn_all = _L0_ffn_setup()
    _L0_ffn_in = {k: v for k, v in _L0_ffn_all.items() if k in ('pos_w', 'pos_b', 'qkv_w', 'qkv_b', 'wo_w', 'wo_b')}
    del _L0_ffn_all
    return {'x': x, 'txt': txt, 'L0_tok_conv_w': _L0_tok_in['conv_w'], 'L0_tok_conv_b': _L0_tok_in['conv_b'], 'L0_tok_gamma': _L0_tok_in['gamma'], 'L0_tok_beta': _L0_tok_in['beta'], 'L0_tok_dense_w': _L0_tok_in['dense_w'], 'L0_tok_dense_b': _L0_tok_in['dense_b'], 'L0_attn_W_in': _L0_attn_in['W_in'], 'L0_attn_b_in': _L0_attn_in['b_in'], 'L0_attn_W_out': _L0_attn_in['W_out'], 'L0_attn_b_out': _L0_attn_in['b_out'], 'L0_ffn_pos_w': _L0_ffn_in['pos_w'], 'L0_ffn_pos_b': _L0_ffn_in['pos_b'], 'L0_ffn_qkv_w': _L0_ffn_in['qkv_w'], 'L0_ffn_qkv_b': _L0_ffn_in['qkv_b'], 'L0_ffn_wo_w': _L0_ffn_in['wo_w'], 'L0_ffn_wo_b': _L0_ffn_in['wo_b']}

def reference(x, txt, L0_tok_conv_w, L0_tok_conv_b, L0_tok_gamma, L0_tok_beta, L0_tok_dense_w, L0_tok_dense_b, L0_attn_W_in, L0_attn_b_in, L0_attn_W_out, L0_attn_b_out, L0_ffn_pos_w, L0_ffn_pos_b, L0_ffn_qkv_w, L0_ffn_qkv_b, L0_ffn_wo_w, L0_ffn_wo_b):
    import jax
    import jax.numpy as jnp

    def _L0_tok_ref(x, conv_w, conv_b, gamma, beta, dense_w, dense_b):
        import jax, jax.numpy as jnp
        import numpy as np
        B, H, W, C = (64, 224, 224, 3)
        P, D = (16, 128)
        LN_EPS = 0.001

        def _shift4(x):
            pad = lambda a, spec: jnp.pad(a, spec)
            right = pad(x[:, :, :-1, :], ((0, 0), (0, 0), (1, 0), (0, 0)))
            left = pad(x[:, :, 1:, :], ((0, 0), (0, 0), (0, 1), (0, 0)))
            down = pad(x[:, :-1, :, :], ((0, 0), (1, 0), (0, 0), (0, 0)))
            up = pad(x[:, 1:, :, :], ((0, 0), (0, 1), (0, 0), (0, 0)))
            return [right, left, down, up]
        xs = jnp.concatenate([x, *_shift4(x)], axis=-1)
        y = jax.lax.conv_general_dilated(xs, conv_w, window_strides=(P, P), padding='VALID', dimension_numbers=('NHWC', 'HWIO', 'NHWC')) + conv_b
        y = y.reshape(y.shape[0], -1, D)
        mu = jnp.mean(y, axis=-1, keepdims=True)
        var = jnp.mean(jnp.square(y - mu), axis=-1, keepdims=True)
        y = (y - mu) * jax.lax.rsqrt(var + LN_EPS) * gamma + beta
        return y @ dense_w + dense_b

    def _L0_attn_ref(x, W_in, b_in, W_out, b_out):
        import jax, jax.numpy as jnp
        import numpy as np
        N_HEADS = 8
        D_K = 64
        NEG = 1000000000.0
        B, L, C = x.shape
        H, Dk = (N_HEADS, D_K)
        scale = Dk ** (-0.5)
        qkv = x @ W_in + b_in
        qkv = qkv.reshape(B, L, H, 3 * Dk)
        q, k, v = jnp.split(qkv, 3, axis=-1)
        attn = jnp.einsum('bihd,bjhd->bijh', q, k) * scale
        mask = jnp.tril(jnp.ones((L, L), dtype=x.dtype))[None, :, :, None]
        attn = attn * mask - NEG * (1.0 - mask)
        attn = jax.nn.softmax(attn, axis=2)
        res = jnp.einsum('bijh,bjhd->bihd', attn, v)
        res = res.reshape(B, L, H * Dk)
        res = res @ W_out + b_out
        return res + x

    def _L0_ffn_ref(x, pos_w, pos_b, qkv_w, qkv_b, wo_w, wo_b):
        import jax, jax.numpy as jnp
        import numpy as np
        from jax import lax
        N, M, DIM, HEADS, TOPK = (4, 512, 128, 8, 16)

        def _split_heads(t, h):
            n, m, c = t.shape
            return t.reshape(n, m, h, c // h).transpose(0, 2, 1, 3).reshape(n * h, m, c // h)
        n, m, c = x.shape
        h = HEADS
        scale = c ** (-0.5)
        pos = lax.conv_general_dilated(x.transpose(0, 2, 1), pos_w, window_strides=(1,), padding=[(1, 1)], feature_group_count=c, dimension_numbers=('NCH', 'OIH', 'NCH'))
        x = x + (pos + pos_b[None, :, None]).transpose(0, 2, 1)
        qkv = x @ qkv_w.T + qkv_b
        q, k, v = jnp.split(qkv, [c, 2 * c], axis=-1)
        q = _split_heads(q, h)
        k = _split_heads(k, h)
        v = _split_heads(v, h)
        qd = lax.stop_gradient(q)
        kd = lax.stop_gradient(k)
        logits = jnp.einsum('bmd,bpd->bmp', qd * scale, kd)
        _, idx = lax.top_k(logits, TOPK)
        gather = jax.vmap(lambda t, i: t[i])
        k_sel = gather(k, idx)
        v_sel = gather(v, idx)
        attn = jax.nn.softmax(jnp.einsum('bmd,bmkd->bmk', q * scale, k_sel), axis=-1)
        out = jnp.einsum('bmk,bmkd->bmd', attn, v_sel)
        d = c // h
        out = out.reshape(n, h, m, d).transpose(0, 2, 1, 3).reshape(n, m, c)
        return out @ wo_w.T + wo_b
    h = _L0_tok_ref(x, L0_tok_conv_w, L0_tok_conv_b, L0_tok_gamma, L0_tok_beta, L0_tok_dense_w, L0_tok_dense_b)
    h = jnp.concatenate([h, txt], axis=1)
    h = h + _L0_attn_ref(_layernorm(h, axis=-1), L0_attn_W_in, L0_attn_b_in, L0_attn_W_out, L0_attn_b_out)
    h = h + _L0_ffn_ref(_layernorm(h, axis=-1), L0_ffn_pos_w, L0_ffn_pos_b, L0_ffn_qkv_w, L0_ffn_qkv_b, L0_ffn_wo_w, L0_ffn_wo_b)
    return h

_drawn_inputs = setup_inputs


def setup_inputs(seed=0):
    import zlib

    import numpy as np

    out = dict(_drawn_inputs(seed))
    spreads = {'L0_tok_conv_b': (0.0, 0.1),
     'L0_tok_gamma': (1.0, 0.2),
     'L0_tok_beta': (0.0, 0.1),
     'L0_tok_dense_b': (0.0, 0.1),
     'L0_attn_b_in': (0.0, 0.1),
     'L0_attn_b_out': (0.0, 0.1)}
    factors = {'L0_ffn_pos_w': 8.0,
     'L0_ffn_pos_b': 8.0,
     'L0_ffn_qkv_w': 2.733,
     'L0_ffn_qkv_b': 8.0,
     'L0_ffn_wo_w': 2.811,
     'L0_ffn_wo_b': 3.601}
    for name, (base, spread) in spreads.items():
        noise = np.random.default_rng([zlib.crc32(name.encode()), seed]).standard_normal(out[name].shape)
        drawn = base * np.exp(spread * noise) if base else spread * noise
        out[name] = jnp.asarray(drawn.astype(out[name].dtype))
    for name, factor in factors.items():
        out[name] = (out[name] * factor).astype(out[name].dtype)
    return out
```

```python
from contextlib import ExitStack

import concourse.bass as bass
from concourse import mybir

B, IMG, CH = 8, 518, 3
P, D = 16, 128
G = (IMG - P) // P + 1
TXT = 77
L = G * G + TXT
NT = (L + 127) // 128
NPT = G * G // 128
LP = NT * 128
LAST = L - (NT - 1) * 128
U = P + 2
UV = U * CH
KU = 2 * UV
NK = U // 2
HA, DK = 8, 64
NP = HA // 2
HF, DF = 8, 16
TOK_EPS, EPS = 1e-3, 1e-5
NEG = -3.0e38
MASK = -1.0e9
SHIFTS = [(1, 1), (1, 0), (1, 2), (0, 1), (2, 1)]
Q_PARTS = [0, 0, 1, 1, 0, 2, 1, 2]
K_PARTS = [0, 1, 0, 1, 2, 0, 2, 1]

def tok_order():
    names = []
    for s in range(NPT + 1):
        if s < NPT:
            names.append(("XT", s))
        if s > 0:
            names.append(("Y", s - 1))
    return names + [("ZT", 0), ("H", 0)]


SECTIONS = [
    ("tok", 1, tok_order()),
    ("x1", 1, ["X1T"]),
    ("pair", NP, ["Q", "K", "V"] + [("S", i) for i in range(2 * NT)]),
    ("out1", 1, [("OT", i) for i in range(NT // 3)] + ["RES"]),
    ("prep", 1, ["X2T", "FQ", "FK", "FV"]),
    ("head", HF, [("L", i) for i in range(NT)]),
    ("out2", 1, ["OCT", "WO"]),
]


def ring_layout():
    where, before, total = {}, {}, [0, 0]
    for sec, reps, names in SECTIONS:
        count = [0, 0]
        for n, name in enumerate(names):
            where[sec, name] = (n % 2, count[n % 2])
            count[n % 2] += 1
        before[sec] = (list(total), count)
        total = [total[i] + reps * count[i] for i in (0, 1)]
    return where, before, total


WHERE, BEFORE, PER_BATCH = ring_layout()


def fill(sec, name, b, it=0):
    buf, k = WHERE[sec, name]
    before, count = BEFORE[sec]
    return buf, b * PER_BATCH[buf] + (it * count[buf] + (before[buf] + k))


def key_groups(n):
    return [(g, min(g + 4, n)) for g in range(0, n, 4)]


def build(nc, x, txt, conv_w, conv_b, gamma, beta, dense_w, dense_b, W_in, b_in, W_out, b_out,
          pos_w, pos_b, qkv_w, qkv_b, wo_w, wo_b, out):
    f32, bf16 = mybir.dt.float32, mybir.dt.bfloat16
    ALU = mybir.AluOpType
    ACT = mybir.ActivationFunctionType
    AX = mybir.AxisListType

    ctx = ExitStack()
    with ctx:
        def sb(name, shape, dt=f32):
            return ctx.enter_context(nc.sbuf_tensor(name, shape, dt))

        def sem(name):
            return ctx.enter_context(nc.semaphore(name))

        ident = sb("ident", [128, 128])
        ident_b = sb("ident_b", [128, 128], bf16)
        mask_b = sb("mask_b", [128, 128], bf16)
        Wf = sb("Wf", [128, NK, D])
        gW = sb("gW", [D, D])
        dW = sb("dW", [D, D])
        dbB = sb("dbB", [128, D])
        convB = sb("convB", [128, D])
        boutB = sb("boutB", [128, D])
        woB = sb("woB", [128, D])
        bvB = sb("bvB", [128, HA, DK])
        fvB = sb("fvB", [128, D])
        cols = sb("cols", [D, 8])
        betaB = sb("betaB", [D, 128])
        bqk = sb("bqk", [128, NP, 2])
        fqk = sb("fqk", [D, 2])
        posw1 = sb("posw1", [D, 1])
        Wo1 = sb("Wo1", [128, 4, D])
        WT = sb("WT", [D, 4, D])
        X = sb("X", [128, NPT, U * UV])
        Wp = sb("Wp", [D, 3, 2, DK])
        O = sb("O", [128, NT, HA, DK])
        stack = sb("stack", [128, 2, HF, LP], bf16)
        qk = sb("qk", [128, 3, LP])
        H = sb("H", [128, NT, D])
        X1 = sb("X1", [128, NT, D])
        H1 = sb("H1", [128, NT, D])
        OUTB = sb("OUTB", [128, NT, D])
        xT = sb("xT", [128, LP])
        xpT = sb("xpT", [128, LP])
        Vf = sb("Vf", [128, NT, HF, DF + 1])
        A = sb("A", [128, 3, L])
        E1 = sb("E1", [128, 3, L])
        E2 = sb("E2", [128, L])
        PT = sb("PT", [128, 2, NT * 128])
        st = sb("st", [128, NT, 6])
        mv = sb("mv", [128, NT, 2])
        rstd = sb("rstd", [128, NT])
        vareps = sb("vareps", [128, NT])
        newton = sb("newton", [128, NT])
        negmax = sb("negmax", [128, 3])
        rowsum = sb("rowsum", [128, 3])
        rinv = sb("rinv", [128, 3])
        top = sb("top", [128, 3, 16])
        negtop = sb("negtop", [128, 3])
        rden = sb("rden", [128, NT])

        stage = stack[:, :, :, :].rearrange("p a h t -> p (a h t)").bitcast(f32)
        fold = stage[:, 0:5 * NK * D].rearrange("p (s t d) -> p s t d", s=5, t=NK)
        rawT = stage[:, 0:4 * D].rearrange("p (s d) -> p s d", s=4)
        OTs = stage[:, 0:4 * NT * 128]
        XT = PT
        Vp = qk[:, 2, :].rearrange("p (t d) -> p t d", t=NT)
        Oflat = O[:, :, :, :].rearrange("p t h d -> p (t h d)")
        parts = Oflat[:, 0:3 * LP].bitcast(bf16).rearrange("p (a s t) -> p a s t", a=2, s=3)
        qkf = qk[:, 0:2, :]
        Oc = X1
        OcT = xT

        ring = [ctx.enter_context(nc.psum_tensor(f"ring{i}", [128, 1536], f32)) for i in (0, 1)]
        pt_ps = ctx.enter_context(nc.psum_tensor("pt_ps", [128, 512], f32))
        out_ps = ctx.enter_context(nc.psum_tensor("out_ps", [128, 512], f32))

        scratch = nc.dram_tensor("qk_parts", (2, 3, D, LP), bf16, kind="Internal").ap()

        w_loaded = sem("w_loaded")
        fold_loaded = sem("fold_loaded")
        zeroed = sem("zeroed")
        consts = sem("consts")
        setup_v = sem("setup_v")
        setup_g = sem("setup_g")
        setup_pe = sem("setup_pe")
        setup_done = sem("setup_done")
        x_loaded = [sem(f"x_loaded{i}") for i in range(NPT)]
        x_ready = sem("x_ready")
        ring_done = [sem("ring_done0"), sem("ring_done1")]
        ring_free = [sem("ring_free0"), sem("ring_free1")]
        z_ready = sem("z_ready")
        seeded = sem("seeded")
        txt_loaded = sem("txt_loaded")
        h_free = sem("h_free")
        ln_v = sem("ln_v")
        x1_ready = sem("x1_ready")
        wp_loaded = sem("wp_loaded")
        wp_free = sem("wp_free")
        rowmax = sem("rowmax")
        pt_done = sem("pt_done")
        pt_free = sem("pt_free")
        sum_done = sem("sum_done")
        sum_free = sem("sum_free")
        recip = sem("recip")
        x2_ready = sem("x2_ready")
        res_v = sem("res_v")
        pos_v = sem("pos_v")
        split_v = sem("split_v")
        parts_stored = sem("parts_stored")
        stacked = sem("stacked")
        top8 = sem("top8")
        cut8 = sem("cut8")
        top16 = sem("top16")
        cut16 = sem("cut16")
        e2 = sem("e2")
        sparse_p = sem("sparse_p")
        fsum_done = sem("fsum_done")
        fsum_free = sem("fsum_free")
        frecip = sem("frecip")
        stored = sem("stored")
        held_v = sem("held_v")
        held_g = sem("held_g")
        held_pe = sem("held_pe")

        PAIR_GROUPS = 2 * sum(len(key_groups(i + 1)) for i in range(NT))
        HEAD_GROUPS = NT * len(key_groups(NT))
        BATCH_GROUPS = NP * PAIR_GROUPS + HF * HEAD_GROUPS

        def pair_group(b, p, n):
            return b * BATCH_GROUPS + (p * PAIR_GROUPS + n)

        def head_group(b, h, n):
            return b * BATCH_GROUPS + (h * HEAD_GROUPS + (NP * PAIR_GROUPS + n))

        def wait_copied(eng, sec, name, b, it=0):
            buf, n = fill(sec, name, b, it)
            eng.wait_ge(ring_free[buf], n + 2)

        def hold(eng, s, value, counter):
            eng.wait_ge(s, value)
            eng.sem_inc(counter, 1)

        conv_v = conv_w.rearrange("h w c d -> w c h d")
        FIRST_LOADS, ALL_LOADS = 18, 20
        ctx.enter_context(nc.allow_non_contiguous_dma(reason="columns of biases, once"))
        block = ctx.enter_context(nc.Block())

        @block.sync
        def _(sp):
            def load(dst, src):
                sp.dma_start(dst, src).then_inc(w_loaded, 16)

            load(dW[:, :], dense_w)
            load(cols[:, 0:1], gamma.rearrange("(p o) -> p o", o=1))
            load(cols[:, 1:2], beta.rearrange("(p o) -> p o", o=1))
            load(cols[:, 2:5], pos_w.rearrange("p o k -> p (o k)"))
            load(cols[:, 5:6], pos_b.rearrange("(p o) -> p o", o=1))
            load(fqk[:, 0:1], qkv_b[0:D].rearrange("(p o) -> p o", o=1))
            load(fqk[:, 1:2], qkv_b[D:2 * D].rearrange("(p o) -> p o", o=1))
            for dst, src in ((dbB, dense_b), (convB, conv_b), (boutB, b_out), (woB, wo_b),
                             (fvB, qkv_b[2 * D:3 * D])):
                load(dst[:, :], src.rearrange("(o n) -> o n", o=1).broadcast_to((128, D)))
            b_view = b_in.rearrange("(h s d) -> s h d", s=3, d=DK)
            load(bvB[:, :, :], b_view[2:3].broadcast_to((128, HA, DK)))
            for hh in range(2):
                for s in range(2):
                    load(bqk[DK * hh:DK * hh + DK, :, s],
                         b_in.rearrange("(p h s d) -> h s d p", p=NP, h=2, s=3)[hh, s])
            load(Wo1[:, :, :], W_out.rearrange("(t p) n -> p t n", p=128))
            sp.wait_ge(zeroed, 1)
            for s, (du, dv) in enumerate(SHIFTS):
                for par in range(2):
                    ph0 = (par - du) % 2
                    t0 = (ph0 + du) // 2
                    for c in range(CH):
                        first = par * UV + dv * CH + c
                        sp.dma_start(fold[first:first + CH * (P - 1) + 1:CH, s, t0:t0 + P // 2, :],
                                     conv_v[:, CH * s + c, ph0::2, :]).then_inc(fold_loaded, 16)
            sp.wait_ge(setup_g, 4)
            load(rawT[:, 0:3, :], qkv_w.rearrange("(s p) n -> p s n", p=128))
            load(rawT[:, 3, :], wo_w)

            x_flat = x.rearrange("b h w c -> b (h w c)")
            win_v = W_in.rearrange("c (p h s d) -> p s c h d", p=NP, h=2, s=3)

            def patches(b, row, rows, j0=0, e0=0, e1=UV):
                start = x_flat[b].offset + (row * IMG * CH + j0 * P * CH - CH + e0)
                return bass.AP(x.tensor, start, [[P * CH, G - j0], [IMG * CH, rows], [1, e1 - e0]])

            sp.sem_inc(stored, 16)

            def load_images(b, first=False):
                for i in range(NPT):
                    if not first:
                        buf, n = fill("tok", ("XT", i), b - 1)
                        sp.wait_ge(ring_done[buf], n + 1)
                    for r in range(4):
                        row = P * (4 * i + r) - 1
                        dst = X[32 * r:32 * r + 32, i, :].rearrange("p (u e) -> p u e", u=U)
                        u0 = 2 if row < 0 else 0
                        sp.dma_start(dst[:, u0:U, :], patches(b, row + u0, U - u0)).then_inc(x_loaded[i], 16)
                        if row < 0:
                            sp.dma_start(dst[:, 1:2, CH:UV], patches(b, 0, 1, 0, CH, UV)).then_inc(x_loaded[i], 16)
                            sp.dma_start(dst[1:G, 1:2, 0:CH], patches(b, 0, 1, 1, 0, CH)).then_inc(x_loaded[i], 16)

            def batch(b, last):
                sp.wait_ge(h_free, b + 1)
                sp.dma_start(H[0:TXT, NT - 1, :], txt[b]).then_inc(txt_loaded, 16)
                with sp.Fori(0, NP) as p:
                    sp.wait_ge(wp_free, b * NP + (p + 1))
                    for s in range(3):
                        sp.dma_start(Wp[:, s, :, :], win_v[p, s]).then_inc(wp_loaded, 16)
                sp.wait_ge(split_v, b * 6 + 6)
                for a in range(2):
                    sp.dma_start(scratch[a].rearrange("s d t -> d s t"), parts[:, a]).then_inc(parts_stored, 16)
                sp.wait_ge(parts_stored, b * 32 + 32)
                for a, which in enumerate((Q_PARTS, K_PARTS)):
                    for r, s in enumerate(which):
                        sp.dma_start(stack[DF * r:DF * r + DF, a, :, :],
                                     scratch[a, s].rearrange("(h d) t -> d h t", h=HF)).then_inc(stacked, 16)
                if not last:
                    load_images(b + 1)
                wait_copied(sp, "out2", "WO", b)
                sp.dma_start(out[b, 0:NPT * 128, :].rearrange("(t p) d -> p t d", p=128),
                             OUTB[:, 0:NPT, :]).then_inc(stored, 16)
                sp.dma_start(out[b, NPT * 128:L, :], OUTB[0:LAST, NT - 1, :]).then_inc(stored, 16)

            load_images(0, first=True)
            with sp.Fori(0, B - 1) as b:
                batch(b, False)
            batch(B - 1, True)
            sp.wait_ge(stored, B * 32 + 16)

        @block.gpsimd
        def _(pool):
            nc.gpsimd.memset(stage[:, 0:5 * NK * D], 0.0).then_inc(zeroed, 1)
            nc.gpsimd.memset(ident[:, :], 0.0).then_inc(held_g, 1)
            nc.gpsimd.memset(mask_b[:, :], 0.0).then_inc(held_g, 1)
            nc.gpsimd.memset(X[0:32, 0, 0:UV], 0.0).then_inc(held_g, 1)
            nc.gpsimd.memset(H[:, NT - 1, :], 0.0).then_inc(h_free, 1)
            nc.gpsimd.memset(xpT[:, L:LP], 0.0).then_inc(held_g, 1)
            nc.gpsimd.memset(Vf[:, :, :, DF:DF + 1], 1.0).then_inc(held_g, 1)
            pool.wait_ge(held_g, 5)
            nc.gpsimd.affine_select(out=ident[:, :], in_=ident[:, :], compare_op=ALU.not_equal, fill=1.0,
                                    base=0, pattern=[[-1, 128]], channel_multiplier=1).then_inc(consts, 1)
            nc.gpsimd.affine_select(out=mask_b[:, :], in_=mask_b[:, :], compare_op=ALU.is_ge, fill=MASK,
                                    base=0, pattern=[[-1, 128]], channel_multiplier=1).then_inc(consts, 1)
            pool.wait_ge(consts, 2)
            nc.gpsimd.tensor_copy(ident_b[:, :], ident[:, :]).then_inc(consts, 1)
            pool.wait_ge(fold_loaded, 16 * 30)
            nc.gpsimd.tensor_tensor(Wf[0:KU], fold[0:KU, 0], fold[0:KU, 1], ALU.add).then_inc(setup_g, 1)
            for s in range(2, 5):
                pool.wait_ge(setup_g, s - 1)
                nc.gpsimd.tensor_tensor(Wf[0:KU], Wf[0:KU], fold[0:KU, s], ALU.add).then_inc(setup_g, 1)

            pool.sem_inc(sparse_p, 1)
            with pool.Fori(0, B) as b:
                hold(pool, sparse_p, b * (HF * NT) + 1, held_g)
                for i in range(NPT):
                    hold(pool, x_loaded[i], b * (96 if i == 0 else 64) + (96 if i == 0 else 64), held_g)
                    for r in range(4):
                        halo = X[32 * r:32 * r + 1, i, :].rearrange("p (u e) -> p u e", u=U)[:, 0:U, 0:CH]
                        last = nc.gpsimd.memset(halo, 0.0)
                    last.then_inc(x_ready, 1)
                with pool.Fori(0, HF) as h:
                    for i in range(NT):
                        T = b * (HF * NT) + (h * NT + i)
                        pool.wait_ge(e2, T + 1)
                        nc.gpsimd.tensor_tensor(A[:, i % 3, :], E1[:, i % 3, :], E2[:, :], ALU.subtract
                                                ).then_inc(sparse_p, 1)

        def pe_fill_wait(pe, sec, name, b, it=0):
            buf, n = fill(sec, name, b, it)
            pe.wait_ge(ring_free[buf], n + 1)
            return ring[buf], ring_done[buf]

        @block.tensor
        def _(pe):
            pe.wait_ge(consts, 3)
            pe.wait_ge(setup_v, 2)
            nc.tensor.matmul(ring[1][:, 0:D], betaB[:, :], dW[:, :], start=True, stop=True).then_inc(setup_pe, 1)
            pe.wait_ge(w_loaded, 16 * ALL_LOADS)
            for s in range(4):
                last = nc.tensor.transpose(ring[0][:, D * s:D * s + D], rawT[:, s, :], ident[:, :])
            last.then_inc(setup_pe, 1)
            pe.wait_ge(setup_done, 2)
            pe.wait_ge(setup_g, 4)
            for s in (0, 1):
                pe.sem_inc(ring_free[s], 1)
            pe.sem_inc(wp_free, 1)
            pe.sem_inc(pt_free, 1)
            pe.sem_inc(sum_free, 1)
            pe.sem_inc(fsum_free, 1)

            def transposes(dst, src_of, n, rows=128):
                for t in range(n):
                    last = nc.tensor.transpose(dst[0:rows, 128 * t:128 * t + 128], src_of(t), ident[:, :])
                return last

            def chunks(width):
                return [(c, min(c + 512, width)) for c in range(0, width, 512)]

            with pe.Fori(0, B) as b:
                for kind, i in tok_order():
                    acc, done = pe_fill_wait(pe, "tok", (kind, i), b)
                    if kind == "XT":
                        pe.wait_ge(x_ready, b * NPT + (i + 1))
                        transposes(acc, lambda t: X[:, i, KU * t:KU * t + KU], NK, KU).then_inc(done, 1)
                    elif kind == "Y":
                        wait_copied(pe, "tok", ("XT", i), b)
                        for t in range(NK):
                            last = nc.tensor.matmul(acc[:, 0:D], XT[0:KU, i % 2, 128 * t:128 * t + 128],
                                                    Wf[0:KU, t, :], start=(t == 0), stop=(t == NK - 1))
                        last.then_inc(done, 1)
                    elif kind == "ZT":
                        pe.wait_ge(z_ready, b + 1)
                        transposes(acc, lambda t: X1[:, t, :], NPT).then_inc(done, 1)
                    else:
                        wait_copied(pe, "tok", ("ZT", 0), b)
                        for t in range(NPT):
                            last = nc.tensor.matmul(acc[:, 128 * t:128 * t + 128], xT[:, 128 * t:128 * t + 128],
                                                    gW[:, :], start=True, stop=True)
                        last.then_inc(done, 1)
                acc, done = pe_fill_wait(pe, "x1", "X1T", b)
                pe.wait_ge(x1_ready, b + 1)
                transposes(acc, lambda t: X1[:, t, :], NT).then_inc(done, 1)
                wait_copied(pe, "x1", "X1T", b)
                pe.sem_inc(held_pe, 1)
                with pe.Fori(0, NP) as p:
                    pe.wait_ge(wp_loaded, b * (NP * 48) + (p * 48 + 48))
                    for s, name in enumerate(("Q", "K")):
                        acc, done = pe_fill_wait(pe, "pair", name, b, p)
                        w = Wp[:, s, :, :].rearrange("c h d -> c (h d)")
                        for c0, c1 in chunks(LP):
                            last = nc.tensor.matmul(acc[:, c0:c1], w, xT[:, c0:c1], start=True, stop=True)
                        last.then_inc(done, 1)
                    acc, done = pe_fill_wait(pe, "pair", "V", b, p)
                    w = Wp[:, 2, :, :].rearrange("c h d -> c (h d)")
                    for t in range(NT):
                        last = nc.tensor.matmul(acc[:, 128 * t:128 * t + 128], xT[:, 128 * t:128 * t + 128], w,
                                                start=True, stop=True)
                    last.then_inc(done, 1)
                    wait_copied(pe, "pair", "Q", b, p)
                    wait_copied(pe, "pair", "K", b, p)

                    def scores(n):
                        hh, i = divmod(n, NT)
                        rows = slice(DK * hh, DK * hh + DK)
                        acc, done = pe_fill_wait(pe, "pair", ("S", n), b, p)
                        width = min(128 * (i + 1), L)
                        for c0, c1 in chunks(width):
                            last = nc.tensor.matmul(acc[:, c0:c1], qk[rows, 0, 128 * i:128 * i + 128],
                                                    qk[rows, 1, c0:c1], start=True, stop=c1 < width)
                            if n == 0 and c0 == 0:
                                last.then_inc(wp_free, 1)
                        last = nc.tensor.matmul(acc[:, 128 * i:width], ident_b[:, :],
                                                mask_b[:, 0:width - 128 * i], start=False, stop=True)
                        last.then_inc(done, 1)

                    scores(0)
                    scores(1)
                    wait_copied(pe, "pair", "V", b, p)
                    g = 0
                    for n in range(2 * NT):
                        hh, i = divmod(n, NT)
                        wait_copied(pe, "pair", ("S", n), b, p)
                        groups = key_groups(i + 1)

                        def sums(k0, k1):
                            for k in range(k0, k1):
                                rows = LAST if k == NT - 1 else 128
                                last = nc.tensor.matmul(out_ps[:, 0:DK], PT[0:rows, n % 2, 128 * k:128 * k + 128],
                                                        Vp[0:rows, k, DK * hh:DK * hh + DK],
                                                        start=(k == 0), stop=(k == i))
                            if k1 == i + 1:
                                last.then_inc(sum_done, 1)

                        for j, (k0, k1) in enumerate(groups):
                            pe.wait_ge(pt_free, pair_group(b, p, g) + 1)
                            for k in range(k0, k1):
                                w = LAST if k == NT - 1 else 128
                                last = nc.tensor.transpose(pt_ps[0:w, 128 * (k - k0):128 * (k - k0) + 128],
                                                           E1[:, n % 3, 128 * k:128 * k + w], ident[:, :])
                            last.then_inc(pt_done, 1)
                            g += 1
                            if j == 0 and n + 2 < 2 * NT:
                                scores(n + 2)
                            if j > 0:
                                if j == 1:
                                    pe.wait_ge(sum_free, b * (NP * 2 * NT) + (p * 2 * NT + n + 1))
                                sums(*groups[j - 1])
                        if len(groups) == 1:
                            pe.wait_ge(sum_free, b * (NP * 2 * NT) + (p * 2 * NT + n + 1))
                        pe.wait_ge(pt_free, pair_group(b, p, g) + 1)
                        sums(*groups[-1])
                pe.wait_ge(sum_free, b * (NP * 2 * NT) + (NP * 2 * NT + 1))
                for f in range(NT // 3):
                    acc, done = pe_fill_wait(pe, "out1", ("OT", f), b)
                    last = transposes(acc, lambda t: Oflat[:, 128 * (12 * f + t):128 * (12 * f + t) + 128], 12)
                    last.then_inc(done, 1)
                acc, done = pe_fill_wait(pe, "out1", "RES", b)
                for f in range(NT // 3):
                    wait_copied(pe, "out1", ("OT", f), b)
                for t in range(NT):
                    for c in range(4):
                        last = nc.tensor.matmul(acc[:, 128 * t:128 * t + 128],
                                                OTs[:, 128 * (4 * t + c):128 * (4 * t + c) + 128], Wo1[:, c, :],
                                                start=(c == 0), stop=(c == 3))
                last.then_inc(done, 1)
                acc, done = pe_fill_wait(pe, "prep", "X2T", b)
                pe.wait_ge(x2_ready, b + 1)
                transposes(acc, lambda t: X1[:, t, :], NT).then_inc(done, 1)
                pe.wait_ge(pos_v, b * 3 + 3)
                for s, name in enumerate(("FQ", "FK")):
                    acc, done = pe_fill_wait(pe, "prep", name, b)
                    for c0, c1 in chunks(LP):
                        last = nc.tensor.matmul(acc[:, c0:c1], WT[:, s, :], xpT[:, c0:c1], start=True, stop=True)
                    last.then_inc(done, 1)
                acc, done = pe_fill_wait(pe, "prep", "FV", b)
                for t in range(NT):
                    last = nc.tensor.matmul(acc[:, 128 * t:128 * t + 128], xpT[:, 128 * t:128 * t + 128],
                                            WT[:, 2, :], start=True, stop=True)
                last.then_inc(done, 1)
                pe.wait_ge(stacked, b * 256 + 256)
                wait_copied(pe, "prep", "FV", b)

                def logits(h, i):
                    acc, done = pe_fill_wait(pe, "head", ("L", i), b, h)
                    for c0, c1 in chunks(L):
                        last = nc.tensor.matmul(acc[:, c0:c1], stack[:, 0, h, 128 * i:128 * i + 128],
                                                stack[:, 1, h, c0:c1], start=True, stop=True)
                    last.then_inc(done, 1)

                def weigh(h, i):
                    pe.wait_ge(sparse_p, b * (HF * NT) + (h * NT + (i + 2)))
                    groups = key_groups(NT)

                    def sums(k0, k1):
                        for k in range(k0, k1):
                            rows = LAST if k == NT - 1 else 128
                            last = nc.tensor.matmul(out_ps[:, (DF + 1) * i:(DF + 1) * (i + 1)],
                                                    PT[0:rows, i % 2, 128 * k:128 * k + 128],
                                                    Vf[0:rows, k, h, :], start=(k == 0), stop=(k == NT - 1))
                        if k1 == NT and i == NT - 1:
                            last.then_inc(fsum_done, 1)

                    for j, (k0, k1) in enumerate(groups):
                        pe.wait_ge(pt_free, head_group(b, h, 3 * i + j) + 1)
                        for k in range(k0, k1):
                            w = LAST if k == NT - 1 else 128
                            last = nc.tensor.transpose(pt_ps[0:w, 128 * (k - k0):128 * (k - k0) + 128],
                                                       A[:, i % 3, 128 * k:128 * k + w], ident[:, :])
                        last.then_inc(pt_done, 1)
                        if j > 0:
                            if i == 0 and j == 1:
                                pe.wait_ge(fsum_free, b * HF + (h + 1))
                            sums(*groups[j - 1])
                    pe.wait_ge(pt_free, head_group(b, h, 3 * i + 3) + 1)
                    sums(*groups[-1])

                def head(h, first):
                    for i in range(NT):
                        logits(h, i)
                        if i >= 3:
                            weigh(h, i - 3)
                        elif not first:
                            weigh(h - 1, i + NT - 3)

                head(0, True)
                with pe.Fori(1, HF) as h:
                    head(h, False)
                for i in range(NT - 3, NT):
                    weigh(HF - 1, i)
                acc, done = pe_fill_wait(pe, "out2", "OCT", b)
                pe.wait_ge(fsum_free, b * HF + (HF + 1))
                transposes(acc, lambda t: Oc[:, t, :], NT).then_inc(done, 1)
                acc, done = pe_fill_wait(pe, "out2", "WO", b)
                wait_copied(pe, "out2", "OCT", b)
                for t in range(NT):
                    last = nc.tensor.matmul(acc[:, 128 * t:128 * t + 128], OcT[:, 128 * t:128 * t + 128],
                                            WT[:, 3, :], start=True, stop=True)
                last.then_inc(done, 1)

        @block.scalar
        def _(act):
            def taken(sec, name, b, it=0):
                buf, n = fill(sec, name, b, it)
                act.wait_ge(ring_done[buf], n + 1)
                return ring[buf], ring_free[buf]

            def seed(b, k, n):
                act.wait_ge(ln_v, b * 21 + (7 * k + 3))
                nc.scalar.activation(rstd[:, 0:n], vareps[:, 0:n], ACT.Ln).then_inc(seeded, 1)
                act.wait_ge(seeded, b * 6 + (2 * k + 1))
                nc.scalar.activation(rstd[:, 0:n], rstd[:, 0:n], ACT.Exp, scale=-0.5).then_inc(seeded, 1)

            with act.Fori(0, B) as b:
                for kind, i in tok_order():
                    if kind == "XT":
                        acc, free = taken("tok", (kind, i), b)
                        nc.scalar.copy(XT[0:KU, i % 2, 0:128 * NK], acc[0:KU, 0:128 * NK]
                                       ).then_inc(free, 1)
                    elif kind == "ZT":
                        seed(b, 0, NPT)
                        acc, free = taken("tok", (kind, i), b)
                        nc.scalar.copy(xT[:, 0:128 * NPT], acc[:, 0:128 * NPT]).then_inc(free, 1)
                seed(b, 1, NT)
                acc, free = taken("x1", "X1T", b)
                nc.scalar.copy(xT[:, :], acc[:, 0:LP]).then_inc(free, 1)
                with act.Fori(0, NP) as p:
                    for s, name in enumerate(("Q", "K")):
                        acc, free = taken("pair", name, b, p)
                        nc.scalar.activation(qk[:, s, :], acc[:, 0:LP], ACT.Identity, bias=bqk[:, p, s:s + 1],
                                             scale=DK ** -0.5 if s == 0 else 1.0).then_inc(free, 1)
                    for n in range(2 * NT):
                        i = n % NT
                        T = b * (NP * 2 * NT) + (p * 2 * NT + n)
                        buf, _n = fill("pair", ("S", n), b, p)
                        act.wait_ge(rowmax, T + 1)
                        width = min(128 * (i + 1), L)
                        nc.scalar.activation(E1[:, n % 3, 0:width], ring[buf][:, 0:width], ACT.Exp,
                                             bias=negmax[:, n % 3:n % 3 + 1], scale=1.0,
                                             accum_out=rowsum[:, n % 3:n % 3 + 1]
                                             ).then_inc(ring_free[buf], 1)
                for f in range(NT // 3):
                    acc, free = taken("out1", ("OT", f), b)
                    nc.scalar.copy(OTs[:, 1536 * f:1536 * f + 1536], acc[:, :]).then_inc(free, 1)
                seed(b, 2, NT)
                acc, free = taken("prep", "X2T", b)
                nc.scalar.copy(xT[:, :], acc[:, 0:LP]).then_inc(free, 1)
                for s, name in enumerate(("FQ", "FK")):
                    acc, free = taken("prep", name, b)
                    scale = D ** -0.5 if s == 0 else 1.0
                    nc.scalar.activation(qkf[:, s, :], acc[:, 0:LP], ACT.Identity, bias=fqk[:, s:s + 1],
                                         scale=scale)
                    nc.scalar.activation(parts[:, s, 0, :], acc[:, 0:LP], ACT.Identity, bias=fqk[:, s:s + 1],
                                         scale=scale).then_inc(free, 1)

                def exp_all(h, i):
                    T = b * (HF * NT) + (h * NT + i)
                    buf, _n = fill("head", ("L", i), b, h)
                    act.wait_ge(cut8, T + 1)
                    nc.scalar.activation(E1[:, i % 3, :], ring[buf][:, 0:L], ACT.Exp,
                                         bias=negtop[:, i % 3:i % 3 + 1], scale=1.0
                                         ).then_inc(ring_free[buf], 1)

                def exp_rest(h, i):
                    T = b * (HF * NT) + (h * NT + i)
                    act.wait_ge(cut16, T + 1)
                    act.wait_ge(sparse_p, T + 1)
                    nc.scalar.activation(E2[:, :], A[:, i % 3, :], ACT.Exp, bias=negtop[:, i % 3:i % 3 + 1],
                                         scale=1.0).then_inc(e2, 1)

                def copy_groups(h, i, which):
                    for j in which:
                        k0, k1 = key_groups(NT)[j]
                        act.wait_ge(pt_done, head_group(b, h, 3 * i + j) + 1)
                        full = k1 - (k1 == NT)
                        if full > k0:
                            last = nc.scalar.copy(PT[:, i % 2, 128 * k0:128 * full], pt_ps[:, 0:128 * (full - k0)])
                        if k1 == NT:
                            o = 128 * (NT - 1 - k0)
                            last = nc.scalar.copy(PT[0:LAST, i % 2, 128 * (NT - 1):LP], pt_ps[0:LAST, o:o + 128])
                        last.then_inc(pt_free, 1)

                def head(h, first):
                    for i in range(NT):
                        old = (h, i - 2) if i >= 2 else (h - 1, i + NT - 2)
                        if i >= 1:
                            exp_rest(h, i - 1)
                        elif not first:
                            exp_rest(h - 1, NT - 1)
                        if i == NT - 1:
                            exp_all(h, i)
                        if i >= 2 or not first:
                            copy_groups(*old, (0, 1))
                        if i < NT - 1:
                            exp_all(h, i)
                        if i >= 2 or not first:
                            copy_groups(*old, (2,))

                head(0, True)
                with act.Fori(1, HF) as h:
                    head(h, False)
                exp_rest(HF - 1, NT - 1)
                for i in range(NT - 2, NT):
                    copy_groups(HF - 1, i, (0, 1, 2))
                acc, free = taken("out2", "OCT", b)
                nc.scalar.copy(OcT[:, :], acc[:, 0:LP]).then_inc(free, 1)

        @block.vector
        def _(dve):
            def taken(sec, name, b, it=0):
                buf, n = fill(sec, name, b, it)
                dve.wait_ge(ring_done[buf], n + 1)
                return ring[buf], ring_free[buf]

            def bcast(row, n):
                return row.unsqueeze(1).broadcast_to((128, n, row.shape[-1]))

            dve.wait_ge(w_loaded, 16 * FIRST_LOADS)
            nc.vector.tensor_copy(betaB[:, :], cols[:, 1:2].broadcast_to((D, 128))).then_inc(setup_v, 1)
            nc.vector.tensor_scalar(gW[:, :], dW[:, :], cols[:, 0:1], None, ALU.mult).then_inc(setup_v, 1)
            nc.vector.tensor_scalar(bqk[:, :, 0], bqk[:, :, 0], DK ** -0.5, None, ALU.mult).then_inc(setup_v, 1)
            nc.vector.tensor_scalar(fqk[:, 0:1], fqk[:, 0:1], D ** -0.5, None, ALU.mult).then_inc(setup_v, 1)
            nc.vector.tensor_scalar(posw1[:, :], cols[:, 3:4], 1.0, None, ALU.add).then_inc(setup_v, 1)
            dve.wait_ge(setup_pe, 1)
            nc.vector.tensor_tensor(dbB[:, :], ring[1][:, 0:D], dbB[:, :], ALU.add).then_inc(setup_done, 1)
            dve.wait_ge(setup_pe, 2)
            nc.vector.tensor_copy(WT[:, :, :].rearrange("p s d -> p (s d)"), ring[0][:, 0:4 * D]
                                  ).then_inc(setup_done, 1)

            def layernorm(src, dst, n, eps, b, k, ready):
                base = 7 * k
                for t in range(n):
                    last = nc.vector.bn_stats(st[:, t, :], src[:, t, :])
                last.then_inc(ln_v, 1)
                hold(dve, ln_v, b * 21 + (base + 1), held_v)
                for t in range(n):
                    last = nc.vector.bn_aggr(mv[:, t, :], st[:, t, :])
                last.then_inc(ln_v, 1)
                dve.wait_ge(ln_v, b * 21 + (base + 2))
                nc.vector.tensor_scalar(vareps[:, 0:n], mv[:, 0:n, 1], eps, None, ALU.add).then_inc(ln_v, 1)
                dve.wait_ge(seeded, b * 6 + (2 * k + 2))
                y, v, w = rstd[:, 0:n], vareps[:, 0:n], newton[:, 0:n]
                nc.vector.tensor_tensor(w, v, y, ALU.mult).then_inc(ln_v, 1)
                dve.wait_ge(ln_v, b * 21 + (base + 4))
                nc.vector.tensor_tensor(w, w, y, ALU.mult).then_inc(ln_v, 1)
                dve.wait_ge(ln_v, b * 21 + (base + 5))
                nc.vector.tensor_scalar(w, w, -0.5, 1.5, ALU.mult, ALU.add).then_inc(ln_v, 1)
                dve.wait_ge(ln_v, b * 21 + (base + 6))
                nc.vector.tensor_tensor(y, y, w, ALU.mult).then_inc(ln_v, 1)
                dve.wait_ge(ln_v, b * 21 + (base + 7))
                for t in range(n):
                    last = nc.vector.tensor_scalar(dst[:, t, :], src[:, t, :], mv[:, t, 0:1], rstd[:, t:t + 1],
                                                   ALU.subtract, ALU.mult)
                last.then_inc(ready, 1)

            with dve.Fori(0, B) as b:
                for i in range(NPT):
                    acc, free = taken("tok", ("Y", i), b)
                    nc.vector.tensor_tensor(H[:, i, :], acc[:, 0:D], convB[:, :], ALU.add).then_inc(free, 1)
                wait_copied(dve, "tok", ("Y", NPT - 2), b)
                wait_copied(dve, "tok", ("Y", NPT - 1), b)
                layernorm(H, X1, NPT, TOK_EPS, b, 0, z_ready)
                acc, free = taken("tok", ("H", 0), b)
                nc.vector.tensor_tensor(H[:, 0:NPT, :], acc[:, 0:NPT * D].rearrange("p (t d) -> p t d", t=NPT),
                                        bcast(dbB[:, :], NPT), ALU.add).then_inc(free, 1)
                dve.wait_ge(txt_loaded, b * 16 + 16)
                wait_copied(dve, "tok", ("H", 0), b)
                layernorm(H, X1, NT, EPS, b, 1, x1_ready)
                dve.wait_ge(x1_ready, b + 1)
                nc.vector.tensor_tensor(H[:, :, :], H[:, :, :], X1[:, :, :], ALU.add).then_inc(res_v, 1)
                dve.wait_ge(res_v, b * 2 + 1)
                nc.vector.tensor_tensor(H[:, :, :], H[:, :, :], bcast(boutB[:, :], NT), ALU.add).then_inc(res_v, 1)
                with dve.Fori(0, NP) as p:
                    acc, free = taken("pair", "V", b, p)
                    bv = bvB[:, :, :].rearrange("p (q h) d -> p q (h d)", q=NP)[:, p, :]
                    nc.vector.tensor_tensor(Vp, acc[:, 0:LP].rearrange("p (t d) -> p t d", t=NT), bcast(bv, NT),
                                            ALU.add).then_inc(free, 1)

                    def row_max(n):
                        acc, _free = taken("pair", ("S", n), b, p)
                        width = min(128 * (n % NT + 1), L)
                        nc.vector.reduce_max(negmax[:, n % 3:n % 3 + 1], acc[:, 0:width], AX.X, negate=True
                                             ).then_inc(rowmax, 1)

                    row_max(0)
                    row_max(1)
                    g = 0
                    for n in range(2 * NT):
                        hh, i = divmod(n, NT)
                        T = b * (NP * 2 * NT) + (p * 2 * NT + n)
                        for j, (k0, k1) in enumerate(key_groups(i + 1)):
                            dve.wait_ge(pt_done, pair_group(b, p, g) + 1)
                            full = k1 - (k1 == NT)
                            if full > k0:
                                last = nc.vector.tensor_copy(PT[:, n % 2, 128 * k0:128 * full],
                                                             pt_ps[:, 0:128 * (full - k0)])
                            if k1 == NT:
                                o = 128 * (NT - 1 - k0)
                                last = nc.vector.tensor_copy(PT[0:LAST, n % 2, 128 * (NT - 1):LP],
                                                             pt_ps[0:LAST, o:o + 128])
                            last.then_inc(pt_free, 1)
                            g += 1
                            if j == 0 and n + 2 < 2 * NT:
                                row_max(n + 2)
                        wait_copied(dve, "pair", ("S", n), b, p)
                        nc.vector.reciprocal(rinv[:, n % 3:n % 3 + 1], rowsum[:, n % 3:n % 3 + 1]).then_inc(recip, 1)
                        dve.wait_ge(recip, T + 1)
                        dve.wait_ge(sum_done, T + 1)
                        o_v = O[:, :, :, :].rearrange("p t (q e) d -> p t q e d", e=2)
                        nc.vector.tensor_scalar(o_v[:, i, p, hh, :], out_ps[:, 0:DK], rinv[:, n % 3:n % 3 + 1],
                                                None, ALU.mult).then_inc(sum_free, 1)
                acc, free = taken("out1", "RES", b)
                dve.wait_ge(res_v, b * 2 + 2)
                nc.vector.tensor_tensor(H1[:, :, :].rearrange("p t d -> p (t d)"), acc[:, 0:LP],
                                        H[:, :, :].rearrange("p t d -> p (t d)"), ALU.add).then_inc(free, 1)
                wait_copied(dve, "out1", "RES", b)
                layernorm(H1, X1, NT, EPS, b, 2, x2_ready)
                dve.wait_ge(x2_ready, b + 1)
                nc.vector.tensor_tensor(H1[:, :, :], H1[:, :, :], bcast(woB[:, :], NT), ALU.add).then_inc(h_free, 1)
                wait_copied(dve, "prep", "X2T", b)
                nc.vector.tensor_scalar(xpT[:, 0:L], xT[:, 0:L], posw1[:, :], cols[:, 5:6], ALU.mult, ALU.add
                                        ).then_inc(pos_v, 1)
                dve.wait_ge(pos_v, b * 3 + 1)
                nc.vector.scalar_tensor_tensor(xpT[:, 1:L], xT[:, 0:L - 1], cols[:, 2:3], xpT[:, 1:L],
                                               ALU.mult, ALU.add).then_inc(pos_v, 1)
                dve.wait_ge(pos_v, b * 3 + 2)
                nc.vector.scalar_tensor_tensor(xpT[:, 0:L - 1], xT[:, 1:L], cols[:, 4:5], xpT[:, 0:L - 1],
                                               ALU.mult, ALU.add).then_inc(pos_v, 1)
                for a, name in enumerate(("FQ", "FK")):
                    wait_copied(dve, "prep", name, b)
                    nc.vector.tensor_tensor(qkf[:, a, :], qkf[:, a, :], parts[:, a, 0, :], ALU.subtract
                                            ).then_inc(split_v, 1)
                    dve.wait_ge(split_v, b * 6 + (3 * a + 1))
                    nc.vector.tensor_copy(parts[:, a, 1, :], qkf[:, a, :]).then_inc(split_v, 1)
                    dve.wait_ge(split_v, b * 6 + (3 * a + 2))
                    nc.vector.tensor_tensor(parts[:, a, 2, :], qkf[:, a, :], parts[:, a, 1, :], ALU.subtract
                                            ).then_inc(split_v, 1)
                acc, free = taken("prep", "FV", b)
                nc.vector.tensor_tensor(
                    Vf[:, :, :, 0:DF], acc[:, 0:LP].rearrange("p (t h d) -> p t h d", t=NT, h=HF),
                    fvB[:, :].rearrange("p (h d) -> p h d", h=HF).unsqueeze(1).broadcast_to((128, NT, HF, DF)),
                    ALU.add).then_inc(free, 1)

                def choose(h, i):
                    T = b * (HF * NT) + (h * NT + i)
                    s = i % 3
                    buf, n = fill("head", ("L", i), b, h)
                    hold(dve, ring_done[buf], n + 1, held_v)
                    nc.vector.max(top[:, s, 0:8], ring[buf][:, 0:L]).then_inc(top8, 1)
                    dve.wait_ge(top8, T + 1)
                    nc.vector.tensor_scalar(negtop[:, s:s + 1], top[:, s, 0:1], -1.0, None, ALU.mult)
                    hold(dve, pt_done, head_group(b, h, 3 * i - 6), held_v)
                    nc.vector.match_replace(A[:, s, :], top[:, s, 0:8], ring[buf][:, 0:L], NEG).then_inc(cut8, 1)
                    hold(dve, cut8, T + 1, held_v)
                    nc.vector.max(top[:, s, 8:16], A[:, s, :]).then_inc(top16, 1)
                    hold(dve, top16, T + 1, held_v)
                    nc.vector.match_replace(A[:, s, :], top[:, s, 8:16], A[:, s, :], NEG).then_inc(cut16, 1)

                def normalise(h):
                    dve.wait_ge(fsum_done, b * HF + (h + 1))
                    sums = out_ps[:, 0:NT * (DF + 1)].rearrange("p (t e) -> p t e", t=NT)
                    nc.vector.reciprocal(rden[:, :], sums[:, :, DF]).then_inc(frecip, 1)
                    dve.wait_ge(frecip, b * HF + (h + 1))
                    nc.vector.tensor_tensor(Oc[:, :, :].rearrange("p t (h d) -> p t h d", h=HF)[:, :, h, :],
                                            sums[:, :, 0:DF], rden[:, :].unsqueeze(2).broadcast_to((128, NT, DF)),
                                            ALU.mult).then_inc(fsum_free, 1)

                for i in range(NT):
                    choose(0, i)
                with dve.Fori(1, HF) as h:
                    for i in range(NT):
                        choose(h, i)
                        if i == 1:
                            normalise(h - 1)
                normalise(HF - 1)
                acc, free = taken("out2", "WO", b)
                dve.wait_ge(stored, b * 32 + 16)
                dve.wait_ge(h_free, b + 2)
                nc.vector.tensor_tensor(OUTB[:, :, :].rearrange("p t d -> p (t d)"), acc[:, 0:LP],
                                        H1[:, :, :].rearrange("p t d -> p (t d)"), ALU.add).then_inc(free, 1)


_INS = ["x", "txt", "L0_tok_conv_w", "L0_tok_conv_b", "L0_tok_gamma", "L0_tok_beta", "L0_tok_dense_w",
        "L0_tok_dense_b", "L0_attn_W_in", "L0_attn_b_in", "L0_attn_W_out", "L0_attn_b_out", "L0_ffn_pos_w",
        "L0_ffn_pos_b", "L0_ffn_qkv_w", "L0_ffn_qkv_b", "L0_ffn_wo_w", "L0_ffn_wo_b"]


def kernel(**inputs):
    import numpy as np
    import concourse.bacc as bacc
    from concourse.bass_utils import run_bass_kernel_spmd as run

    nc = bacc.Bacc("TRN2", target_bir_lowering=False, num_devices=1)
    arrays, args = {}, []
    for name in _INS:
        a = np.ascontiguousarray(inputs[name])
        arrays[f"in_{name}"] = a
        args.append(nc.dram_tensor(f"in_{name}", a.shape, mybir.dt.from_np(a.dtype), kind="ExternalInput").ap())
    args.append(nc.dram_tensor("out_0", (B, L, D), mybir.dt.float32, kind="ExternalOutput").ap())
    build(nc, *args)
    r = run(nc, [arrays], core_ids=[0])
    return r.results[0]["out_0"]
```

```python
from contextlib import ExitStack

import concourse.bass as bass
from concourse import mybir

B, IMG, CH = 8, 518, 3
P, D = 16, 128
G = (IMG - P) // P + 1
TXT = 77
L = G * G + TXT
NT = (L + 127) // 128
NPT = G * G // 128
LP = NT * 128
LAST = L - (NT - 1) * 128
U = P + 2
UV = U * CH
KU = 2 * UV
NK = U // 2
HA, DK = 8, 64
NP = HA // 2
HF, DF = 8, 16
TOK_EPS, EPS = 1e-3, 1e-5
NEG = -3.0e38
MASK = -1.0e9
SHIFTS = [(1, 1), (1, 0), (1, 2), (0, 1), (2, 1)]
Q_PARTS = [0, 0, 1, 1, 0, 2, 1, 2]
K_PARTS = [0, 1, 0, 1, 2, 0, 2, 1]

def tok_order():
    names = []
    for s in range(NPT + 1):
        if s < NPT:
            names.append(("XT", s))
        if s > 0:
            names.append(("Y", s - 1))
    return names + [("ZT", 0), ("H", 0)]


FILLS = (tok_order() + ["X1T"] + [("OT", i) for i in range(NT // 3)] + ["RES"] + ["X2T", "FQ", "FK", "FV"])
PER_CYCLE = [(len(FILLS) + 1) // 2, len(FILLS) // 2]


def fill(name, c):
    n = FILLS.index(name)
    return n % 2, c * PER_CYCLE[n % 2] + n // 2


STEPS = 2 * NT
TILES = {2 + (NT - 1) * hh + max(i - 1, 0): [] for hh in range(2) for i in range(NT)}
for _hh in range(2):
    for _i in range(NT):
        TILES[2 + (NT - 1) * _hh + max(_i - 1, 0)].append(NT * _hh + _i)
NB = len(TILES)
HALF = 512
MAIN = 2 * HALF
TAIL = L - MAIN


def blocks(step):
    return [(t, k, HALF * j + 128 * k) for j, t in enumerate(TILES[step]) for k in range(t % NT + 1)]


def fours(items):
    return [items[g:g + 4] for g in range(0, len(items), 4)]


WG = fours(range(NT))


def step_events(n, sparse, causal, carried_sparse, carried_causal):
    w, sw = ([(e, n - 2, j) for j in range(len(WG))] for e in ("turn_sparse", "sum_sparse"))
    if not (sparse if n >= 2 else carried_sparse):
        w = sw = [None] * len(WG)

    def causal_groups(step):
        live = (causal and step in TILES) or (carried_causal and step < 0)
        return len(fours(blocks(step % STEPS))) if live else 0

    c = [("turn_causal", n - 1, j) for j in range(causal_groups(n - 1))] + 3 * [None]
    sc = [("sum_causal", n - 1, j) for j in range(causal_groups(n - 1))] + [None]
    ev = [("logits", n, 0) if sparse else None]
    ev += [("sum_causal", n - 2, j) for j in range(1, causal_groups(n - 2))]
    ev += [w[0], w[1],
          ("proj_q", 0, 0) if causal and n == 0 else None,
          ("proj_v", 0, 0) if causal and n == 1 else None,
          ("scores", n, 0) if causal and n in TILES else None,
          sw[0], w[2], sw[1], c[0], sw[2], ("join_sums", n - 2, 0) if sw[0] else None,
          ("exp_all", n, 0) if sparse else None,
          c[1], sc[0], c[2],
          ("proj_k", 0, 0) if causal and n == 0 else None,
          ("proj_last", 0, 0) if causal and n == 1 else None,
          ("exp_causal", n, 0) if causal and n in TILES else None]
    return [e for e in ev if e]


def count_groups(event, n):
    if event == "scores":
        return int(TILES[n][0] % NT == NT - 1)
    return {"turn_causal": 1, "turn_sparse": 1, "proj_last": 2}.get(event, 0)


def number_groups(start, steps, *kind):
    at = {}
    for n in range(steps):
        for event in step_events(n, *kind):
            at[event] = start
            start += count_groups(*event[:2])
    return at, start


def round_groups(sparse, causal):
    return (number_groups(0, STEPS, sparse, causal, False, False)[1],
            number_groups(0, STEPS, sparse, causal, sparse, causal)[1])


def groups_before(c, p):
    own = round_groups(c != 0 if isinstance(c, int) else True, c != B if isinstance(c, int) else True)[1]
    full, alone = round_groups(True, True)[1], round_groups(False, True)[1]
    assert full % 2 == 0 and alone % 2 == 0 and own % 2 == 0
    before = 0 if isinstance(c, int) and c == 0 else (c - 1) * (NP * full) + NP * alone
    return before if isinstance(p, int) and p == 0 else before + (p - 1) * own


def plan(c, p, sparse, causal, carried):
    first = round_groups(sparse, causal)[0]
    kind = (sparse, causal, sparse and carried, causal and carried)
    steps = STEPS
    if isinstance(p, int) and p == NP:
        kind, steps = (False, False, sparse, causal), 2
    at, _end = number_groups(first if carried else 0, steps, *kind)
    if kind[3]:
        last, end = number_groups(0, STEPS, sparse, causal, False, False)
        for event, n, j in list(last):
            if event == "turn_causal" and n == STEPS - 2:
                at[event, -2, j] = first + last[event, n, j] - end
    return steps, kind, at, groups_before(c, p)


def build(nc, x, txt, conv_w, conv_b, gamma, beta, dense_w, dense_b, W_in, b_in, W_out, b_out,
          pos_w, pos_b, qkv_w, qkv_b, wo_w, wo_b, out):
    f32, bf16 = mybir.dt.float32, mybir.dt.bfloat16
    ALU = mybir.AluOpType
    ACT = mybir.ActivationFunctionType
    AX = mybir.AxisListType

    ctx = ExitStack()
    with ctx:
        def sb(name, shape, dt=f32):
            return ctx.enter_context(nc.sbuf_tensor(name, shape, dt))

        def sem(name):
            return ctx.enter_context(nc.semaphore(name))

        ident = sb("ident", [128, 128])
        ident_b = sb("ident_b", [128, 128], bf16)
        mask_b = sb("mask_b", [128, 128], bf16)
        Wf = sb("Wf", [128, NK, D])
        gW = sb("gW", [D, D])
        dW = sb("dW", [D, D])
        dbB = sb("dbB", [128, D])
        convB = sb("convB", [128, D])
        boutB = sb("boutB", [128, D])
        woB = sb("woB", [128, D])
        cols = sb("cols", [D, 8])
        bqkv = sb("bqkv", [128, NP, 3])
        fqkv = sb("fqkv", [D, 3])
        posw1 = sb("posw1", [D, 1])
        Wo1 = sb("Wo1", [128, 4, D])
        WT = sb("WT", [D, 4, D])
        X = sb("X", [128, NPT, U * UV])
        Wp = sb("Wp", [D, 3, 2, DK])
        O = sb("O", [128, NT, HA, DK])
        stack = sb("stack", [128, 2, HF, LP], bf16)
        qk = sb("qk", [128, 3, LP])
        H = sb("H", [128, NT, D])
        X1 = sb("X1", [128, NT, D])
        H1 = sb("H1", [128, NT, D])
        OUTB = sb("OUTB", [128, NT, D])
        xT = sb("xT", [128, LP])
        xpT = sb("xpT", [128, LP])
        Vf = sb("Vf", [128, NT, HF, DF + 1])
        A = sb("A", [128, 3, L])
        Vh = sb("Vh", [128, 2, NT, 32])
        split = sb("split", [128, 128])
        join = sb("join", [128, DF + 1])
        E1 = sb("E1", [128, 2, LP])
        PB = sb("PB", [128, LP])
        tail = sb("tail", [128, TAIL])
        PT = sb("PT", [128, 2, NT * 128])
        st = sb("st", [128, NT, 6])
        mv = sb("mv", [128, NT, 2])
        rstd = sb("rstd", [128, NT])
        vareps = sb("vareps", [128, NT])
        newton = sb("newton", [128, NT])
        negmax = sb("negmax", [128, 2, 2])
        negparts = sb("negparts", [128, 2])
        rowsum = sb("rowsum", [128, 2, 2])
        rinv = sb("rinv", [128, 2, 2])
        top = sb("top", [128, 3, 16])
        negtop = sb("negtop", [128, 3])
        rden = sb("rden", [128, NT])

        stage = stack[:, :, :, :].rearrange("p a h t -> p (a h t)").bitcast(f32)
        fold = stage[:, 0:5 * NK * D].rearrange("p (s t d) -> p s t d", s=5, t=NK)
        rawT = stage[:, 0:4 * D].rearrange("p (s d) -> p s d", s=4)
        OTs = stage[:, 0:4 * NT * 128]
        XT = PT
        columns = E1[:, :, :].rearrange("p a t -> p (a t)")[:, 0:6 * 128].rearrange("p (s n) -> p s n", s=6)
        Vp = qk[:, 2, :].rearrange("p (t d) -> p t d", t=NT)
        Oflat = O[:, :, :, :].rearrange("p t h d -> p (t h d)")
        parts = Oflat[:, 0:3 * LP].bitcast(bf16).rearrange("p (a s t) -> p a s t", a=2, s=3)
        qkf = qk[:, 0:2, :]
        Oc = X1
        OcT = xT

        logit_ps = ctx.enter_context(nc.psum_tensor("logit_ps", [128, 3 * HALF], f32))
        causal_ps = ctx.enter_context(nc.psum_tensor("causal_ps", [128, 4 * HALF], f32))
        out_ps = ctx.enter_context(nc.psum_tensor("out_ps", [128, HALF], f32))
        ring = [logit_ps, causal_ps]
        score_ps = causal_ps[:, 0:MAIN]
        turn_ps = [causal_ps[:, MAIN + HALF * i:MAIN + HALF * i + HALF] for i in (0, 1)]
        causal_sums = out_ps[:, 0:2 * DK]
        split_sums = out_ps[:, 3 * 128:4 * 128]
        sparse_sums = out_ps[:, 2 * DK:2 * DK + NT * (DF + 1)].rearrange("p (t e) -> p t e", t=NT)

        scratch = nc.dram_tensor("qk_parts", (2, 3, D, LP), bf16, kind="Internal").ap()

        w_loaded = sem("w_loaded")
        fold_loaded = sem("fold_loaded")
        zeroed = sem("zeroed")
        consts = sem("consts")
        setup_v = sem("setup_v")
        setup_g = sem("setup_g")
        setup_pe = sem("setup_pe")
        setup_done = sem("setup_done")
        x_loaded = [sem(f"x_loaded{i}") for i in range(NPT)]
        x_ready = sem("x_ready")
        ring_done = [sem("ring_done0"), sem("ring_done1")]
        ring_free = [sem("ring_free0"), sem("ring_free1")]
        z_ready = sem("z_ready")
        seeded = sem("seeded")
        txt_loaded = sem("txt_loaded")
        h_free = sem("h_free")
        ln_v = sem("ln_v")
        x1_ready = sem("x1_ready")
        x2_ready = sem("x2_ready")
        res_v = sem("res_v")
        wp_loaded = sem("wp_loaded")
        wp_free = sem("wp_free")
        score_done = sem("score_done")
        score_free = sem("score_free")
        rowmax = sem("rowmax")
        turn_done = sem("turn_done")
        turn_free = sem("turn_free")
        sum_done = sem("sum_done")
        sum_free = sem("sum_free")
        causal_v = sem("causal_v")
        pos_v = sem("pos_v")
        split_v = sem("split_v")
        parts_stored = sem("parts_stored")
        stacked = sem("stacked")
        logit_done = sem("logit_done")
        logit_free = sem("logit_free")
        top8 = sem("top8")
        cut8 = sem("cut8")
        top16 = sem("top16")
        cut16 = sem("cut16")
        marked = sem("marked")
        chosen = sem("chosen")
        v_ready = sem("v_ready")
        split_done = sem("split_done")
        split_copied = sem("split_copied")
        weighed = sem("weighed")
        head_free = sem("head_free")
        frecip = sem("frecip")
        out2_done = sem("out2_done")
        out2_free = sem("out2_free")
        stored = sem("stored")
        held_v = sem("held_v")
        held_g = sem("held_g")
        held_pe = sem("held_pe")
        held_a = sem("held_a")

        def wait_copied(eng, name, c):
            buf, n = fill(name, c)
            eng.wait_ge(ring_free[buf], n + 2)

        def score_number(c, p, n):
            return c * (NP * (3 + NB)) + (p * (3 + NB) + n)

        def causal_step(c, p, step):
            return c * (NP * NB) + (p * NB + (step - 2 if step >= 0 else step))

        def step_scores(c, p, step):
            return c * (NP * (3 + NB)) + (p * (3 + NB) + (step + 1 if step >= 0 else step))

        def sparse_tile(c, p, n):
            return (c - 1) * (HF * NT) + (p * STEPS + n)

        def sums_read(m):
            return m - 2 if m - 2 in TILES or m < 2 else -1

        def hold(eng, s, value, counter):
            eng.wait_ge(s, value)
            eng.sem_inc(counter, 1)

        conv_v = conv_w.rearrange("h w c d -> w c h d")
        FIRST_LOADS, ALL_LOADS = 17, 19
        ctx.enter_context(nc.allow_non_contiguous_dma(reason="columns of biases, once"))
        block = ctx.enter_context(nc.Block())

        @block.sync
        def _(sp):
            def load(dst, src):
                sp.dma_start(dst, src).then_inc(w_loaded, 16)

            load(dW[:, :], dense_w)
            load(cols[:, 0:1], gamma.rearrange("(p o) -> p o", o=1))
            load(cols[:, 1:2], beta.rearrange("(p o) -> p o", o=1))
            load(cols[:, 2:5], pos_w.rearrange("p o k -> p (o k)"))
            load(cols[:, 5:6], pos_b.rearrange("(p o) -> p o", o=1))
            load(fqkv[:, :], qkv_b.rearrange("(s p) -> p s", p=D))
            for dst, src in ((dbB, dense_b), (convB, conv_b), (boutB, b_out), (woB, wo_b)):
                load(dst[:, :], src.rearrange("(o n) -> o n", o=1).broadcast_to((128, D)))
            for hh in range(2):
                for s in range(3):
                    load(bqkv[DK * hh:DK * hh + DK, :, s],
                         b_in.rearrange("(p h s d) -> h s d p", p=NP, h=2, s=3)[hh, s])
            load(Wo1[:, :, :], W_out.rearrange("(t p) n -> p t n", p=128))
            sp.wait_ge(zeroed, 1)
            for s, (du, dv) in enumerate(SHIFTS):
                for par in range(2):
                    ph0 = (par - du) % 2
                    t0 = (ph0 + du) // 2
                    for c in range(CH):
                        first = par * UV + dv * CH + c
                        sp.dma_start(fold[first:first + CH * (P - 1) + 1:CH, s, t0:t0 + P // 2, :],
                                     conv_v[:, CH * s + c, ph0::2, :]).then_inc(fold_loaded, 16)
            sp.wait_ge(setup_g, 4)
            load(rawT[:, 0:3, :], qkv_w.rearrange("(s p) n -> p s n", p=128))
            load(rawT[:, 3, :], wo_w)

            x_flat = x.rearrange("b h w c -> b (h w c)")
            win_v = W_in.rearrange("c (p h s d) -> p s c h d", p=NP, h=2, s=3)

            def patches(b, row, rows, j0=0, e0=0, e1=UV):
                start = x_flat[b].offset + (row * IMG * CH + j0 * P * CH - CH + e0)
                return bass.AP(x.tensor, start, [[P * CH, G - j0], [IMG * CH, rows], [1, e1 - e0]])

            sp.sem_inc(stored, 16)

            def load_images(c, first=False):
                for i in range(NPT):
                    if not first:
                        buf, n = fill(("XT", i), c - 1)
                        sp.wait_ge(ring_done[buf], n + 1)
                    for r in range(4):
                        row = P * (4 * i + r) - 1
                        dst = X[32 * r:32 * r + 32, i, :].rearrange("p (u e) -> p u e", u=U)
                        u0 = 2 if row < 0 else 0
                        sp.dma_start(dst[:, u0:U, :], patches(c, row + u0, U - u0)).then_inc(x_loaded[i], 16)
                        if row < 0:
                            sp.dma_start(dst[:, 1:2, CH:UV], patches(c, 0, 1, 0, CH, UV)).then_inc(x_loaded[i], 16)
                            sp.dma_start(dst[1:G, 1:2, 0:CH], patches(c, 0, 1, 1, 0, CH)).then_inc(x_loaded[i], 16)

            def store(b):
                sp.wait_ge(out2_free, b * 2 + 3)
                sp.dma_start(out[b, 0:NPT * 128, :].rearrange("(t p) d -> p t d", p=128),
                             OUTB[:, 0:NPT, :]).then_inc(stored, 16)
                sp.dma_start(out[b, NPT * 128:L, :], OUTB[0:LAST, NT - 1, :]).then_inc(stored, 16)

            def cycle(c, first, last):
                sp.wait_ge(h_free, c + 1)
                sp.dma_start(H[0:TXT, NT - 1, :], txt[c]).then_inc(txt_loaded, 16)
                with sp.Fori(0, NP) as p:
                    sp.wait_ge(wp_free, c * NP + (p + 1))
                    for s in range(3):
                        sp.dma_start(Wp[:, s, :, :], win_v[p, s]).then_inc(wp_loaded, 16)
                if not last:
                    load_images(c + 1)
                if not first:
                    store(c - 1)
                sp.wait_ge(split_v, c * 6 + 6)
                for a in range(2):
                    sp.dma_start(scratch[a].rearrange("s d t -> d s t"), parts[:, a]).then_inc(parts_stored, 16)
                sp.wait_ge(parts_stored, c * 32 + 32)
                for a, which in enumerate((Q_PARTS, K_PARTS)):
                    for r, s in enumerate(which):
                        sp.dma_start(stack[DF * r:DF * r + DF, a, :, :],
                                     scratch[a, s].rearrange("(h d) t -> d h t", h=HF)).then_inc(stacked, 16)

            load_images(0, first=True)
            cycle(0, True, False)
            with sp.Fori(1, B - 1) as c:
                cycle(c, False, False)
            cycle(B - 1, False, True)
            store(B - 1)
            sp.wait_ge(stored, B * 32 + 16)

        @block.gpsimd
        def _(pool):
            nc.gpsimd.memset(stage[:, 0:5 * NK * D], 0.0).then_inc(zeroed, 1)
            nc.gpsimd.memset(ident[:, :], 0.0).then_inc(held_g, 1)
            nc.gpsimd.memset(mask_b[:, :], 0.0).then_inc(held_g, 1)
            nc.gpsimd.memset(X[0:32, 0, 0:UV], 0.0).then_inc(held_g, 1)
            nc.gpsimd.memset(H[:, NT - 1, :], 0.0).then_inc(h_free, 1)
            nc.gpsimd.memset(xpT[:, L:LP], 0.0).then_inc(held_g, 1)
            nc.gpsimd.memset(Vf[:, :, :, DF:DF + 1], 1.0).then_inc(held_g, 1)
            nc.gpsimd.memset(Vh[:, :, :, :], 0.0).then_inc(held_g, 1)
            pool.wait_ge(held_g, 6)
            nc.gpsimd.affine_select(out=ident[:, :], in_=ident[:, :], compare_op=ALU.not_equal, fill=1.0,
                                    base=0, pattern=[[-1, 128]], channel_multiplier=1).then_inc(consts, 1)
            nc.gpsimd.affine_select(out=mask_b[:, :], in_=mask_b[:, :], compare_op=ALU.is_ge, fill=MASK,
                                    base=0, pattern=[[-1, 128]], channel_multiplier=1).then_inc(consts, 1)
            pool.wait_ge(consts, 2)
            for j in range(4):
                nc.gpsimd.tensor_copy(join[32 * j:32 * j + 32, :], ident[32 * j:32 * j + 32, 32 * j:32 * j + DF + 1]
                                      ).then_inc(consts, 1)
                pool.wait_ge(consts, 3 + j)
            nc.gpsimd.tensor_copy(ident_b[:, :], ident[:, :]).then_inc(consts, 1)
            pool.wait_ge(fold_loaded, 16 * 30)
            nc.gpsimd.tensor_tensor(Wf[0:KU], fold[0:KU, 0], fold[0:KU, 1], ALU.add).then_inc(setup_g, 1)
            for s in range(2, 5):
                pool.wait_ge(setup_g, s - 1)
                nc.gpsimd.tensor_tensor(Wf[0:KU], Wf[0:KU], fold[0:KU, s], ALU.add).then_inc(setup_g, 1)

            pool.sem_inc(chosen, 2)

            def halos(c):
                if not (isinstance(c, int) and c == 0):
                    hold(pool, chosen, (c - 1) * (HF * NT) + 2, held_g)
                for i in range(NPT):
                    each = 96 if i == 0 else 64
                    hold(pool, x_loaded[i], c * each + each, held_g)
                    for r in range(4):
                        halo = X[32 * r:32 * r + 1, i, :].rearrange("p (u e) -> p u e", u=U)[:, 0:U, 0:CH]
                        last = nc.gpsimd.memset(halo, 0.0)
                    last.then_inc(x_ready, 1)
                hold(pool, x_ready, c * NPT + NPT, held_g)

            def weights(c):
                wait_copied(pool, "FV", c - 1)
                pool.sem_inc(held_g, 1)
                with pool.Fori(0, NP) as p:
                    for k in range(STEPS):
                        if k in (0, 3):
                            hh = k // 3
                            hold(pool, weighed, sparse_tile(c, p, hh * NT) + 1, held_g)
                            nc.gpsimd.tensor_copy(Vh[:, hh, :, 0:DF + 1], Vf[:, :, 2 * p + hh, :]
                                                  ).then_inc(v_ready, 1)
                        hold(pool, cut16, sparse_tile(c, p, k) + 1, held_g)
                        nc.gpsimd.tensor_scalar(A[:, k % 3, :], A[:, k % 3, :], NEG, None, ALU.is_equal
                                                ).then_inc(marked, 1)
                        pool.wait_ge(logit_free, sparse_tile(c, p, k) + 2)
                        hold(pool, marked, sparse_tile(c, p, k) + 1, held_g)
                        nc.gpsimd.tensor_tensor(A[:, k % 3, :], A[:, k % 3, :], E1[:, k % 2, 0:L], ALU.mult
                                                ).then_inc(chosen, 1)

            halos(0)
            with pool.Fori(1, B) as c:
                halos(c)
                weights(c)
            weights(B)

        def fill_wait(pe, name, c):
            buf, n = fill(name, c)
            pe.wait_ge(ring_free[buf], n + 1)
            return ring[buf], ring_done[buf]

        def chunks(start, width):
            cuts = [start] + [x for x in range(HALF, 3 * HALF, HALF) if start < x < start + width] + [start + width]
            return list(zip(cuts, cuts[1:]))

        @block.tensor
        def _(pe):
            def transposes(dst, src_of, n, rows=128):
                for t in range(n):
                    last = nc.tensor.transpose(dst[0:rows, 128 * t:128 * t + 128], src_of(t), ident[:, :])
                return last

            pe.wait_ge(consts, 7)
            pe.wait_ge(setup_v, 3)
            nc.tensor.matmul(ring[1][:, 0:D], columns[:, 0, :], dW[:, :], start=True, stop=True)
            for q in range(NP):
                last = nc.tensor.matmul(ring[1][:, HALF:HALF + D], columns[:, 1 + q, :], Wo1[:, q, :],
                                        start=(q == 0), stop=(q == NP - 1))
            last.then_inc(setup_pe, 1)
            pe.wait_ge(w_loaded, 16 * ALL_LOADS)
            for s in range(4):
                last = nc.tensor.transpose(ring[0][:, D * s:D * s + D], rawT[:, s, :], ident[:, :])
            last.then_inc(setup_pe, 1)
            pe.wait_ge(setup_done, 3)
            nc.tensor.matmul(out_ps[:, 0:D], columns[:, 5, :], WT[:, 3, :], start=True, stop=True
                             ).then_inc(setup_pe, 1)
            pe.wait_ge(setup_done, 4)
            pe.wait_ge(setup_g, 4)
            for free in (*ring_free, wp_free, score_free, sum_free, logit_free, head_free, out2_free):
                pe.sem_inc(free, 1)
            pe.sem_inc(turn_free, 2)
            pe.sem_inc(weighed, NT + 1)

            def tokens(c):
                for name in tok_order():
                    kind, i = name
                    acc, done = fill_wait(pe, name, c)
                    if kind == "XT":
                        pe.wait_ge(x_ready, c * NPT + (i + 1))
                        transposes(acc, lambda t: X[:, i, KU * t:KU * t + KU], NK, KU).then_inc(done, 1)
                    elif kind == "Y":
                        wait_copied(pe, ("XT", i), c)
                        for t in range(NK):
                            last = nc.tensor.matmul(acc[:, 0:D], XT[0:KU, i % 2, 128 * t:128 * t + 128],
                                                    Wf[0:KU, t, :], start=(t == 0), stop=(t == NK - 1))
                        last.then_inc(done, 1)
                    elif kind == "ZT":
                        pe.wait_ge(z_ready, c + 1)
                        transposes(acc, lambda t: X1[:, t, :], NPT).then_inc(done, 1)
                    else:
                        wait_copied(pe, ("ZT", 0), c)
                        for t in range(NPT):
                            last = nc.tensor.matmul(acc[:, 128 * t:128 * t + 128], xT[:, 128 * t:128 * t + 128],
                                                    gW[:, :], start=True, stop=True)
                        last.then_inc(done, 1)
                acc, done = fill_wait(pe, "X1T", c)
                pe.wait_ge(x1_ready, c + 1)
                transposes(acc, lambda t: X1[:, t, :], NT).then_inc(done, 1)
                wait_copied(pe, "X1T", c)
                pe.sem_inc(held_pe, 1)

            def turn(base, n, srcs, ptlen=None):
                pe.wait_ge(turn_free, base + (n + 1))
                bank = turn_ps[n % 2]
                for j, src in enumerate(srcs):
                    w = src.shape[-1]
                    last = nc.tensor.transpose(bank[0:w, 128 * j:128 * j + 128], src, ident[:, :])
                last.then_inc(turn_done, 1)

            def copied(base, n):
                pe.wait_ge(turn_free, base + (n + 3))

            def a_round(c, p, sparse, causal, carried):
                steps, kind, at, base = plan(c, p, sparse, causal, carried)
                for m in range(steps):
                    for key in step_events(m, *kind):
                        tensor_event(c, p, m, key, sparse, causal, at, base)

            def tensor_event(c, p, m, key, sparse, causal, at, base):
                event, n, j = key
                if event == "logits":
                    pe.wait_ge(logit_free, sparse_tile(c, p, n) + 1)
                    h, i = 2 * p + n // NT, n % NT
                    for c0, c1 in chunks(0, L):
                        last = nc.tensor.matmul(logit_ps[:, c0:c1], stack[:, 0, h, 128 * i:128 * i + 128],
                                                stack[:, 1, h, c0:c1], start=True, stop=True)
                    last.then_inc(logit_done, 1)
                elif event in ("proj_q", "proj_k"):
                    s = int(event == "proj_k")
                    if s == 0:
                        pe.wait_ge(wp_loaded, c * (NP * 48) + (p * 48 + 48))
                    pe.wait_ge(score_free, score_number(c, p, s) + 1)
                    w = Wp[:, s, :, :].rearrange("c h d -> c (h d)")
                    for c0, c1 in chunks(0, MAIN):
                        last = nc.tensor.matmul(score_ps[:, c0:c1], w, xT[:, c0:c1], start=True, stop=True)
                    last.then_inc(score_done, 1)
                elif event == "proj_v":
                    pe.wait_ge(score_free, score_number(c, p, 2) + 1)
                    w = Wp[:, 2, :, :].rearrange("c h d -> c (h d)")
                    for t in range(NPT):
                        last = nc.tensor.matmul(score_ps[:, 128 * t:128 * t + 128],
                                                xT[:, 128 * t:128 * t + 128], w, start=True, stop=True)
                    last.then_inc(score_done, 1)
                elif event == "proj_last":
                    g = at[key]
                    pe.wait_ge(turn_free, base + (g + 1))
                    for s in range(2):
                        w = Wp[:, s, :, :].rearrange("c h d -> c (h d)")
                        last = nc.tensor.matmul(turn_ps[g % 2][:, 128 * s:128 * s + 128], w, xT[:, MAIN:LP],
                                                start=True, stop=True)
                    last.then_inc(turn_done, 1)
                    pe.wait_ge(turn_free, base + (g + 2))
                    w = Wp[:, 2, :, :].rearrange("c h d -> c (h d)")
                    nc.tensor.matmul(turn_ps[(g + 1) % 2][:, 0:128], xT[:, MAIN:LP], w, start=True, stop=True
                                     ).then_inc(turn_done, 1)
                elif event == "scores":
                    order = n - 2
                    if order == 0:
                        copied(base, at["proj_last", 0, 0] + 1)
                    pe.wait_ge(score_free, score_number(c, p, 3 + order) + 1)
                    for j, t in enumerate(TILES[n]):
                        hh, i = divmod(t, NT)
                        rows = slice(DK * hh, DK * hh + DK)
                        q = qk[rows, 0, 128 * i:128 * i + 128]
                        if i == NT - 1:
                            g = at[key]
                            pe.wait_ge(turn_free, base + (g + 1))
                            bank = turn_ps[g % 2]
                            nc.tensor.matmul(bank[:, 0:TAIL], q, qk[rows, 1, MAIN:L], start=True, stop=False)
                            nc.tensor.matmul(bank[:, 0:TAIL], ident_b[:, :], mask_b[:, 0:TAIL],
                                             start=False, stop=True).then_inc(turn_done, 1)
                        width = min(128 * (i + 1), MAIN)
                        for c0, c1 in chunks(HALF * j, width):
                            diagonal = i < NT - 1 and c1 == HALF * j + width
                            last = nc.tensor.matmul(score_ps[:, c0:c1], q,
                                                    qk[rows, 1, c0 - HALF * j:c1 - HALF * j],
                                                    start=True, stop=not diagonal)
                            if order == 0 and j == 0:
                                last.then_inc(wp_free, 1)
                        if i < NT - 1:
                            d0 = HALF * j + 128 * i
                            last = nc.tensor.matmul(score_ps[:, d0:d0 + 128], ident_b[:, :], mask_b[:, :],
                                                    start=False, stop=True)
                    last.then_inc(score_done, 1)
                elif event == "turn_sparse":
                    if j == 0:
                        pe.wait_ge(chosen, sparse_tile(c, p, n) + 3)
                    turn(base, at[key], [A[:, n % 3, 128 * k:min(128 * k + 128, L)] for k in WG[j]])
                elif event == "sum_sparse":
                    i, h = n % NT, n // NT
                    if j == 0 and causal:
                        pe.wait_ge(sum_free, causal_step(c, p, sums_read(m)) + 2)
                    if j == 0 and i == 0:
                        pe.wait_ge(head_free, (c - 1) * HF + (2 * p + (n // NT + 1)))
                        pe.wait_ge(v_ready, (c - 1) * HF + (2 * p + (n // NT + 1)))
                    copied(base, at["turn_sparse", n, j])
                    for q, k in enumerate(WG[j]):
                        rows = LAST if k == NT - 1 else 128
                        last = nc.tensor.matmul(split_sums[32 * q:32 * q + 32, :], Vh[0:rows, h % 2, k, :],
                                                PT[0:rows, 0, 128 * k:128 * k + 128],
                                                start=(k < 4), stop=(k + 4 >= NT))
                    if j == len(WG) - 1:
                        last.then_inc(split_done, 1)
                elif event == "join_sums":
                    pe.wait_ge(split_copied, sparse_tile(c, p, n) + 1)
                    nc.tensor.matmul(sparse_sums[:, n % NT, :], split[:, :], join[:, :], start=True, stop=True
                                     ).then_inc(weighed, 1)
                elif event == "turn_causal":
                    if j == 0:
                        pe.wait_ge(score_free, step_scores(c, p, n) + 2)
                    turn(base, at[key], [PB[:, o:o + (LAST if k == NT - 1 else 128)]
                                         for _t, k, o in fours(blocks(n % STEPS))[j]])
                elif event == "sum_causal":
                    if j == 0:
                        pe.wait_ge(sum_free, causal_step(c, p, n) + 1)
                    copied(base, at["turn_causal", n, j])
                    groups = fours(blocks(n % STEPS))
                    for q, (t, k, _o) in enumerate(groups[j]):
                        hh, i = divmod(t, NT)
                        o = DK * TILES[n % STEPS].index(t)
                        rows = LAST if k == NT - 1 else 128
                        last = nc.tensor.matmul(causal_sums[:, o:o + DK],
                                                PT[0:rows, 1, 512 * j + 128 * q:512 * j + 128 * q + 128],
                                                Vp[0:rows, k, DK * hh:DK * hh + DK],
                                                start=(k == 0), stop=(k == i))
                    if j == len(groups) - 1:
                        last.then_inc(sum_done, 1)

            def output(c):
                pe.wait_ge(head_free, (c - 1) * HF + (HF + 1))
                transposes(ring[0], lambda t: Oc[:, t, :], NT).then_inc(out2_done, 1)
                pe.wait_ge(out2_free, (c - 1) * 2 + 2)
                for t in range(NT):
                    last = nc.tensor.matmul(ring[1][:, 128 * t:128 * t + 128], OcT[:, 128 * t:128 * t + 128],
                                            WT[:, 3, :], start=True, stop=True)
                last.then_inc(out2_done, 1)

            def projections(c, first):
                pe.wait_ge(sum_free, c * (NP * NB) + (NP * NB + 1))
                if not first:
                    pe.wait_ge(out2_free, (c - 1) * 2 + 3)
                for f in range(NT // 3):
                    acc, done = fill_wait(pe, ("OT", f), c)
                    transposes(acc, lambda t: Oflat[:, 128 * (12 * f + t):128 * (12 * f + t) + 128], 12
                               ).then_inc(done, 1)
                acc, done = fill_wait(pe, "RES", c)
                for t in range(NT):
                    if t % 3 == 0:
                        wait_copied(pe, ("OT", t // 3), c)
                    for q in range(NP):
                        last = nc.tensor.matmul(acc[:, 128 * t:128 * t + 128],
                                                OTs[:, 128 * (4 * t + q):128 * (4 * t + q) + 128], Wo1[:, q, :],
                                                start=(q == 0), stop=(q == NP - 1))
                last.then_inc(done, 1)
                acc, done = fill_wait(pe, "X2T", c)
                pe.wait_ge(x2_ready, c + 1)
                transposes(acc, lambda t: X1[:, t, :], NT).then_inc(done, 1)
                pe.wait_ge(pos_v, c * 3 + 3)
                for s, name in enumerate(("FQ", "FK")):
                    acc, done = fill_wait(pe, name, c)
                    for c0, c1 in chunks(0, LP):
                        last = nc.tensor.matmul(acc[:, c0:c1], WT[:, s, :], xpT[:, c0:c1], start=True, stop=True)
                    last.then_inc(done, 1)
                acc, done = fill_wait(pe, "FV", c)
                for t in range(NT):
                    last = nc.tensor.matmul(acc[:, 128 * t:128 * t + 128], xpT[:, 128 * t:128 * t + 128],
                                            WT[:, 2, :], start=True, stop=True)
                last.then_inc(done, 1)

            def sparse_inputs(c):
                pe.wait_ge(stacked, (c - 1) * 256 + 256)
                wait_copied(pe, "FV", c - 1)

            tokens(0)
            a_round(0, 0, False, True, False)
            with pe.Fori(1, NP) as p:
                a_round(0, p, False, True, True)
            a_round(0, NP, False, True, True)
            projections(0, True)
            with pe.Fori(1, B) as c:
                tokens(c)
                sparse_inputs(c)
                a_round(c, 0, True, True, False)
                with pe.Fori(1, NP) as p:
                    a_round(c, p, True, True, True)
                a_round(c, NP, True, True, True)
                output(c)
                projections(c, False)
            sparse_inputs(B)
            a_round(B, 0, True, False, False)
            with pe.Fori(1, NP) as p:
                a_round(B, p, True, False, True)
            a_round(B, NP, True, False, True)
            output(B)

        @block.scalar
        def _(act):
            def taken(name, c):
                buf, n = fill(name, c)
                act.wait_ge(ring_done[buf], n + 1)
                return ring[buf], ring_free[buf]

            def seed(c, k, n):
                act.wait_ge(ln_v, c * 21 + (7 * k + 3))
                nc.scalar.activation(rstd[:, 0:n], vareps[:, 0:n], ACT.Ln).then_inc(seeded, 1)
                act.wait_ge(seeded, c * 6 + (2 * k + 1))
                nc.scalar.activation(rstd[:, 0:n], rstd[:, 0:n], ACT.Exp, scale=-0.5).then_inc(seeded, 1)

            def tokens(c):
                for i in range(NPT):
                    acc, free = taken(("XT", i), c)
                    nc.scalar.copy(XT[0:KU, i % 2, 0:128 * NK], acc[0:KU, 0:128 * NK]).then_inc(free, 1)
                seed(c, 0, NPT)
                acc, free = taken(("ZT", 0), c)
                nc.scalar.copy(xT[:, 0:128 * NPT], acc[:, 0:128 * NPT]).then_inc(free, 1)
                seed(c, 1, NT)
                acc, free = taken("X1T", c)
                nc.scalar.copy(xT[:, :], acc[:, 0:LP]).then_inc(free, 1)

            def copy_turned(bank, slot, q0, tiles):
                short = tiles[-1] == NT - 1
                full = len(tiles) - short
                if full:
                    last = nc.scalar.copy(PT[:, slot, 128 * q0:128 * (q0 + full)], bank[:, 0:128 * full])
                if short:
                    o = 128 * (q0 + full)
                    last = nc.scalar.copy(PT[0:LAST, slot, o:o + 128], bank[0:LAST, 128 * full:128 * full + 128])
                last.then_inc(turn_free, 1)

            def a_round(c, p, sparse, causal, carried):
                steps, kind, at, base = plan(c, p, sparse, causal, carried)

                def turned(g):
                    act.wait_ge(turn_done, base + (g + 1))
                    return turn_ps[g % 2]

                def projected(s):
                    hold(act, score_done, score_number(c, p, s) + 1, held_a)

                for key in [e for m in range(steps) for e in step_events(m, *kind)]:
                    event, n, j = key
                    if event == "turn_sparse":
                        copy_turned(turned(at[key]), 0, 4 * j, WG[j])
                    elif event == "join_sums":
                        act.wait_ge(split_done, sparse_tile(c, p, n) + 1)
                        nc.scalar.copy(split[:, :], split_sums).then_inc(split_copied, 1)
                    elif event == "turn_causal":
                        copy_turned(turned(at[key]), 1, 4 * j, [k for _t, k, _o in fours(blocks(n % STEPS))[j]])
                    elif event == "proj_q":
                        projected(0)
                        nc.scalar.activation(qk[:, 0, 0:MAIN], score_ps, ACT.Identity, bias=bqkv[:, p, 0:1],
                                             scale=DK ** -0.5).then_inc(score_free, 1)
                    elif event == "proj_v":
                        projected(2)
                        nc.scalar.copy(qk[:, 2, 0:MAIN], score_ps).then_inc(score_free, 1)
                    elif event == "proj_k":
                        projected(1)
                        nc.scalar.activation(qk[:, 1, 0:MAIN], score_ps, ACT.Identity, bias=bqkv[:, p, 1:2],
                                             scale=1.0).then_inc(score_free, 1)
                    elif event == "proj_last":
                        bank = turned(at[key])
                        act.sem_inc(held_a, 1)
                        nc.scalar.activation(qk[:, 0, MAIN:LP], bank[:, 0:128], ACT.Identity,
                                             bias=bqkv[:, p, 0:1], scale=DK ** -0.5)
                        nc.scalar.activation(qk[:, 1, MAIN:LP], bank[:, 128:256], ACT.Identity,
                                             bias=bqkv[:, p, 1:2], scale=1.0).then_inc(turn_free, 1)
                        nc.scalar.copy(qk[:, 2, MAIN:LP], turned(at[key] + 1)[:, 0:128]).then_inc(turn_free, 1)
                    elif event == "scores" and count_groups(event, n):
                        nc.scalar.copy(tail[:, :], turned(at[key])[:, 0:TAIL]).then_inc(turn_free, 1)
                    elif event == "exp_all":
                        act.wait_ge(chosen, sparse_tile(c, p, n) + 1)
                        act.wait_ge(cut8, sparse_tile(c, p, n) + 1)
                        nc.scalar.activation(E1[:, n % 2, 0:L], logit_ps[:, 0:L], ACT.Exp,
                                             bias=negtop[:, n % 3:n % 3 + 1], scale=1.0).then_inc(logit_free, 1)
                    elif event == "exp_causal":
                        act.wait_ge(rowmax, causal_step(c, p, n) + 1)
                        s = n % 2
                        if TILES[n][0] % NT == NT - 1:
                            nc.scalar.activation(PB[:, MAIN:L], tail[:, :], ACT.Exp, bias=negmax[:, s, 0:1],
                                                 scale=1.0, accum_out=rowsum[:, s, 1:2])
                        for j, t in enumerate(TILES[n]):
                            o, width = HALF * j, min(128 * (t % NT + 1), MAIN)
                            last = nc.scalar.activation(PB[:, o:o + width], score_ps[:, o:o + width], ACT.Exp,
                                                        bias=negmax[:, s, j:j + 1], scale=1.0,
                                                        accum_out=rowsum[:, s, j:j + 1])
                        last.then_inc(score_free, 1)

            def output(c):
                act.wait_ge(out2_done, (c - 1) * 2 + 1)
                nc.scalar.copy(OcT[:, :], ring[0][:, 0:LP]).then_inc(out2_free, 1)

            def projections(c):
                for f in range(NT // 3):
                    acc, free = taken(("OT", f), c)
                    nc.scalar.copy(OTs[:, 1536 * f:1536 * f + 1536], acc[:, 0:1536]).then_inc(free, 1)
                seed(c, 2, NT)
                acc, free = taken("X2T", c)
                nc.scalar.copy(xT[:, :], acc[:, 0:LP]).then_inc(free, 1)
                for s, name in enumerate(("FQ", "FK")):
                    acc, free = taken(name, c)
                    scale = D ** -0.5 if s == 0 else 1.0
                    nc.scalar.activation(qkf[:, s, :], acc[:, 0:LP], ACT.Identity, bias=fqkv[:, s:s + 1],
                                         scale=scale)
                    nc.scalar.activation(parts[:, s, 0, :], acc[:, 0:LP], ACT.Identity, bias=fqkv[:, s:s + 1],
                                         scale=scale).then_inc(free, 1)
                acc, free = taken("FV", c)
                nc.scalar.copy(Vf[:, :, :, 0:DF], acc[:, 0:LP].rearrange("p (t h d) -> p t h d", t=NT, h=HF)
                               ).then_inc(free, 1)

            nc.scalar.preload_act_table_set("natural_log_exp_and_others")
            tokens(0)
            a_round(0, 0, False, True, False)
            with act.Fori(1, NP) as p:
                a_round(0, p, False, True, True)
            a_round(0, NP, False, True, True)
            projections(0)
            with act.Fori(1, B) as c:
                tokens(c)
                a_round(c, 0, True, True, False)
                with act.Fori(1, NP) as p:
                    a_round(c, p, True, True, True)
                a_round(c, NP, True, True, True)
                output(c)
                projections(c)
            a_round(B, 0, True, False, False)
            with act.Fori(1, NP) as p:
                a_round(B, p, True, False, True)
            a_round(B, NP, True, False, True)
            output(B)

        @block.vector
        def _(dve):
            def taken(name, c):
                buf, n = fill(name, c)
                dve.wait_ge(ring_done[buf], n + 1)
                return ring[buf], ring_free[buf]

            def bcast(row, n):
                return row.unsqueeze(1).broadcast_to((128, n, row.shape[-1]))

            dve.wait_ge(w_loaded, 16 * FIRST_LOADS)
            nc.vector.tensor_copy(columns[:, 0, :], cols[:, 1:2].broadcast_to((D, 128))).then_inc(setup_v, 1)
            for q in range(NP):
                last = nc.vector.tensor_copy(columns[:, 1 + q, :], bqkv[:, q, 2:3].broadcast_to((128, 128)))
            last.then_inc(setup_v, 1)
            nc.vector.tensor_copy(columns[:, 5, :], fqkv[:, 2:3].broadcast_to((128, 128))).then_inc(setup_v, 1)
            nc.vector.tensor_scalar(gW[:, :], dW[:, :], cols[:, 0:1], None, ALU.mult).then_inc(setup_v, 1)
            nc.vector.tensor_scalar(bqkv[:, :, 0], bqkv[:, :, 0], DK ** -0.5, None, ALU.mult).then_inc(setup_v, 1)
            nc.vector.tensor_scalar(fqkv[:, 0:1], fqkv[:, 0:1], D ** -0.5, None, ALU.mult).then_inc(setup_v, 1)
            nc.vector.tensor_scalar(posw1[:, :], cols[:, 3:4], 1.0, None, ALU.add).then_inc(setup_v, 1)
            dve.wait_ge(setup_pe, 1)
            nc.vector.tensor_tensor(dbB[:, :], ring[1][:, 0:D], dbB[:, :], ALU.add).then_inc(setup_done, 1)
            nc.vector.tensor_tensor(boutB[:, :], ring[1][:, HALF:HALF + D], boutB[:, :], ALU.add
                                    ).then_inc(setup_done, 1)
            dve.wait_ge(setup_pe, 2)
            nc.vector.tensor_copy(WT[:, :, :].rearrange("p s d -> p (s d)"), ring[0][:, 0:4 * D]
                                  ).then_inc(setup_done, 1)
            dve.wait_ge(setup_pe, 3)
            nc.vector.tensor_tensor(woB[:, :], out_ps[:, 0:D], woB[:, :], ALU.add).then_inc(setup_done, 1)

            def layernorm(src, dst, n, eps, c, k, ready):
                base = 7 * k
                for t in range(n):
                    last = nc.vector.bn_stats(st[:, t, :], src[:, t, :])
                last.then_inc(ln_v, 1)
                hold(dve, ln_v, c * 21 + (base + 1), held_v)
                for t in range(n):
                    last = nc.vector.bn_aggr(mv[:, t, :], st[:, t, :])
                last.then_inc(ln_v, 1)
                dve.wait_ge(ln_v, c * 21 + (base + 2))
                nc.vector.tensor_scalar(vareps[:, 0:n], mv[:, 0:n, 1], eps, None, ALU.add).then_inc(ln_v, 1)
                dve.wait_ge(seeded, c * 6 + (2 * k + 2))
                y, v, w = rstd[:, 0:n], vareps[:, 0:n], newton[:, 0:n]
                nc.vector.tensor_tensor(w, v, y, ALU.mult).then_inc(ln_v, 1)
                dve.wait_ge(ln_v, c * 21 + (base + 4))
                nc.vector.tensor_tensor(w, w, y, ALU.mult).then_inc(ln_v, 1)
                dve.wait_ge(ln_v, c * 21 + (base + 5))
                nc.vector.tensor_scalar(w, w, -0.5, 1.5, ALU.mult, ALU.add).then_inc(ln_v, 1)
                dve.wait_ge(ln_v, c * 21 + (base + 6))
                nc.vector.tensor_tensor(y, y, w, ALU.mult).then_inc(ln_v, 1)
                dve.wait_ge(ln_v, c * 21 + (base + 7))
                for t in range(n):
                    last = nc.vector.tensor_scalar(dst[:, t, :], src[:, t, :], mv[:, t, 0:1], rstd[:, t:t + 1],
                                                   ALU.subtract, ALU.mult)
                last.then_inc(ready, 1)

            def tokens(c):
                for i in range(NPT):
                    acc, free = taken(("Y", i), c)
                    nc.vector.tensor_tensor(H[:, i, :], acc[:, 0:D], convB[:, :], ALU.add).then_inc(free, 1)
                wait_copied(dve, ("Y", NPT - 2), c)
                wait_copied(dve, ("Y", NPT - 1), c)
                layernorm(H, X1, NPT, TOK_EPS, c, 0, z_ready)
                acc, free = taken(("H", 0), c)
                nc.vector.tensor_tensor(H[:, 0:NPT, :], acc[:, 0:NPT * D].rearrange("p (t d) -> p t d", t=NPT),
                                        bcast(dbB[:, :], NPT), ALU.add).then_inc(free, 1)
                dve.wait_ge(txt_loaded, c * 16 + 16)
                wait_copied(dve, ("H", 0), c)
                layernorm(H, X1, NT, EPS, c, 1, x1_ready)
                dve.wait_ge(x1_ready, c + 1)
                nc.vector.tensor_tensor(H[:, :, :], H[:, :, :], X1[:, :, :], ALU.add).then_inc(res_v, 1)
                dve.wait_ge(res_v, c * 2 + 1)
                nc.vector.tensor_tensor(H[:, :, :], H[:, :, :], bcast(boutB[:, :], NT), ALU.add).then_inc(res_v, 1)

            SMALL = 2 * 2 + NB + 2
            CARRIED = 3

            def a_round(c, p, sparse, causal, carried):
                steps, kind, at, base = plan(c, p, sparse, causal, carried)
                sparse, causal = kind[0], kind[1]
                small = [-CARRIED if kind[3] else 0]

                def step(ins):
                    ins.then_inc(causal_v, 1)
                    small[0] += 1

                def wait_step():
                    dve.wait_ge(causal_v, c * (NP * SMALL) + (p * SMALL + small[0]))

                def row_max(n):
                    s = n % 2
                    dve.wait_ge(score_done, step_scores(c, p, n) + 1)
                    if TILES[n][0] % NT == NT - 1:
                        step(nc.vector.reduce_max(negparts[:, 0:1], score_ps, AX.X, negate=True))
                        dve.wait_ge(turn_free, base + (at["scores", n, 0] + 3))
                        step(nc.vector.reduce_max(negparts[:, 1:2], tail[:, :], AX.X, negate=True))
                        wait_step()
                        last = nc.vector.tensor_tensor(negmax[:, s, 0:1], negparts[:, 0:1], negparts[:, 1:2],
                                                       ALU.min)
                    else:
                        for j, t in enumerate(TILES[n]):
                            o, width = HALF * j, 128 * (t % NT + 1)
                            last = nc.vector.reduce_max(negmax[:, s, j:j + 1], score_ps[:, o:o + width], AX.X,
                                                        negate=True)
                    last.then_inc(rowmax, 1)

                def causal_scale(n):
                    s, tiles = n % 2, TILES[n % STEPS]
                    dve.wait_ge(score_free, step_scores(c, p, n) + 2)
                    if tiles[0] % NT == NT - 1:
                        step(nc.vector.tensor_tensor(rowsum[:, s, 0:1], rowsum[:, s, 0:1], rowsum[:, s, 1:2],
                                                     ALU.add))
                        wait_step()
                    step(nc.vector.reciprocal(rinv[:, s, 0:len(tiles)], rowsum[:, s, 0:len(tiles)]))

                def causal_out(n):
                    s, tiles = n % 2, TILES[n % STEPS]
                    wait_step()
                    dve.wait_ge(sum_done, causal_step(c, p, n) + 1)
                    pair = p if n >= 0 else p - 1
                    o_v = O[:, :, :, :].rearrange("p t (q e) d -> p t q e d", e=2)
                    for j, t in enumerate(tiles):
                        hh, i = divmod(t, NT)
                        last = nc.vector.tensor_scalar(o_v[:, i, pair, hh, :], causal_sums[:, DK * j:DK * j + DK],
                                                       rinv[:, s, j:j + 1], None, ALU.mult)
                    last.then_inc(sum_free, 1)

                for n in range(steps):
                    s = n % 3
                    T = sparse_tile(c, p, n) if sparse else None
                    out = kind[3] if n < 2 else causal and n - 2 in TILES
                    if sparse:
                        hold(dve, logit_done, T + 1, held_v)
                        nc.vector.max(top[:, s, 0:8], logit_ps[:, 0:L]).then_inc(top8, 1)
                    if out:
                        causal_scale(n - 2)
                    if sparse:
                        dve.wait_ge(top8, T + 1)
                        nc.vector.tensor_scalar(negtop[:, s:s + 1], top[:, s, 0:1], -1.0, None, ALU.mult)
                    if out:
                        causal_out(n - 2)
                    if n == 2 and kind[2]:
                        normalise(c, 2 * p - 1)
                    if n == NT + 2 and sparse:
                        normalise(c, 2 * p)
                    if sparse:
                        if n >= 3 or kind[2]:
                            hold(dve, weighed, T - 2 + (NT + 1), held_v)
                        nc.vector.match_replace(A[:, s, :], top[:, s, 0:8], logit_ps[:, 0:L], NEG
                                                ).then_inc(cut8, 1)
                    if sparse:
                        hold(dve, cut8, T + 1, held_v)
                        nc.vector.max(top[:, s, 8:16], A[:, s, :]).then_inc(top16, 1)
                    if causal and n in TILES:
                        row_max(n)
                    if sparse:
                        hold(dve, top16, T + 1, held_v)
                        nc.vector.match_replace(A[:, s, :], top[:, s, 8:16], A[:, s, :], NEG).then_inc(cut16, 1)

            def normalise(c, h):
                dve.wait_ge(weighed, (c - 1) * (HF * NT) + (h * NT + 2 * NT + 1))
                nc.vector.reciprocal(rden[:, :], sparse_sums[:, :, DF]).then_inc(frecip, 1)
                dve.wait_ge(frecip, (c - 1) * HF + (h + 1))
                nc.vector.tensor_tensor(Oc[:, :, :].rearrange("p t (h d) -> p t h d", h=HF)[:, :, h, :],
                                        sparse_sums[:, :, 0:DF], rden[:, :].unsqueeze(2).broadcast_to((128, NT, DF)),
                                        ALU.mult).then_inc(head_free, 1)

            def output(c):
                normalise(c, HF - 1)
                dve.wait_ge(out2_done, (c - 1) * 2 + 2)
                dve.wait_ge(stored, (c - 1) * 32 + 16)
                dve.wait_ge(h_free, (c - 1) + 2)
                nc.vector.tensor_tensor(OUTB[:, :, :].rearrange("p t d -> p (t d)"), ring[1][:, 0:LP],
                                        H1[:, :, :].rearrange("p t d -> p (t d)"), ALU.add).then_inc(out2_free, 1)

            def projections(c):
                acc, free = taken("RES", c)
                dve.wait_ge(res_v, c * 2 + 2)
                nc.vector.tensor_tensor(H1[:, :, :].rearrange("p t d -> p (t d)"), acc[:, 0:LP],
                                        H[:, :, :].rearrange("p t d -> p (t d)"), ALU.add).then_inc(free, 1)
                wait_copied(dve, "RES", c)
                layernorm(H1, X1, NT, EPS, c, 2, x2_ready)
                dve.wait_ge(x2_ready, c + 1)
                nc.vector.tensor_tensor(H1[:, :, :], H1[:, :, :], bcast(woB[:, :], NT), ALU.add).then_inc(h_free, 1)
                wait_copied(dve, "X2T", c)
                nc.vector.tensor_scalar(xpT[:, 0:L], xT[:, 0:L], posw1[:, :], cols[:, 5:6], ALU.mult, ALU.add
                                        ).then_inc(pos_v, 1)
                dve.wait_ge(pos_v, c * 3 + 1)
                nc.vector.scalar_tensor_tensor(xpT[:, 1:L], xT[:, 0:L - 1], cols[:, 2:3], xpT[:, 1:L],
                                               ALU.mult, ALU.add).then_inc(pos_v, 1)
                dve.wait_ge(pos_v, c * 3 + 2)
                nc.vector.scalar_tensor_tensor(xpT[:, 0:L - 1], xT[:, 1:L], cols[:, 4:5], xpT[:, 0:L - 1],
                                               ALU.mult, ALU.add).then_inc(pos_v, 1)
                for a, name in enumerate(("FQ", "FK")):
                    wait_copied(dve, name, c)
                    nc.vector.tensor_tensor(qkf[:, a, :], qkf[:, a, :], parts[:, a, 0, :], ALU.subtract
                                            ).then_inc(split_v, 1)
                    dve.wait_ge(split_v, c * 6 + (3 * a + 1))
                    nc.vector.tensor_copy(parts[:, a, 1, :], qkf[:, a, :]).then_inc(split_v, 1)
                    dve.wait_ge(split_v, c * 6 + (3 * a + 2))
                    nc.vector.tensor_tensor(parts[:, a, 2, :], qkf[:, a, :], parts[:, a, 1, :], ALU.subtract
                                            ).then_inc(split_v, 1)

            tokens(0)
            a_round(0, 0, False, True, False)
            with dve.Fori(1, NP) as p:
                a_round(0, p, False, True, True)
            a_round(0, NP, False, True, True)
            projections(0)
            with dve.Fori(1, B) as c:
                tokens(c)
                a_round(c, 0, True, True, False)
                with dve.Fori(1, NP) as p:
                    a_round(c, p, True, True, True)
                a_round(c, NP, True, True, True)
                output(c)
                projections(c)
            a_round(B, 0, True, False, False)
            with dve.Fori(1, NP) as p:
                a_round(B, p, True, False, True)
            a_round(B, NP, True, False, True)
            output(B)


_INS = ["x", "txt", "L0_tok_conv_w", "L0_tok_conv_b", "L0_tok_gamma", "L0_tok_beta", "L0_tok_dense_w",
        "L0_tok_dense_b", "L0_attn_W_in", "L0_attn_b_in", "L0_attn_W_out", "L0_attn_b_out", "L0_ffn_pos_w",
        "L0_ffn_pos_b", "L0_ffn_qkv_w", "L0_ffn_qkv_b", "L0_ffn_wo_w", "L0_ffn_wo_b"]


def kernel(**inputs):
    import numpy as np
    import concourse.bacc as bacc
    from concourse.bass_utils import run_bass_kernel_spmd as run

    nc = bacc.Bacc("TRN2", target_bir_lowering=False, num_devices=1)
    arrays, args = {}, []
    for name in _INS:
        a = np.ascontiguousarray(inputs[name])
        arrays[f"in_{name}"] = a
        args.append(nc.dram_tensor(f"in_{name}", a.shape, mybir.dt.from_np(a.dtype), kind="ExternalInput").ap())
    args.append(nc.dram_tensor("out_0", (B, L, D), mybir.dt.float32, kind="ExternalOutput").ap())
    build(nc, *args)
    r = run(nc, [arrays], core_ids=[0])
    return r.results[0]["out_0"]
```
